# Optimizing a Trainium2 kernel written in Bass

```python
import numpy as np
import jax
import jax.numpy as jnp

def _softmax(x, axis=-1):
    return jax.nn.softmax(x, axis=axis)
def _gelu(x):
    return jax.nn.gelu(x, approximate=True)
def _silu(x):
    return jax.nn.silu(x)
def _sigmoid(x):
    return jax.nn.sigmoid(x)
def _layernorm(x, axis=-1, eps=1e-5):
    m = jnp.mean(x, axis=axis, keepdims=True)
    v = jnp.var(x, axis=axis, keepdims=True)
    return (x - m) / jnp.sqrt(v + eps)
def _scatter_add(tgt, idx, src, axis=0):
    return tgt.at[idx].add(src)
def _segment_sum(src, seg, n):
    return jax.ops.segment_sum(src, seg, n)

kernel_name = 'mk_metaformer_d1_conv_nchw128_6168dc'

def setup_inputs(seed: int = 0):
    np.random.seed(seed)
    _w = jnp.asarray
    def _rec_inputs():
        import jax
        import jax.numpy as jnp
        _gk = jax.random.key(seed)
        x = 7.22e-05 + 1 * jax.random.normal(jax.random.fold_in(_gk, 1), (4, 128, 128, 128), jnp.float32)
        return x
    x = _rec_inputs()
    def _L0_conv_setup():
        import jax, jax.numpy as jnp
        import numpy as np
        DIM = 128
        HID = 4 * DIM
        EPS = 1e-05

        def _ln(x, g, b):
            mu = jnp.mean(x, axis=-1, keepdims=True)
            var = jnp.mean(jnp.square(x - mu), axis=-1, keepdims=True)
            return (x - mu) * jax.lax.rsqrt(var + EPS) * g + b

        def _block(x, ln0_g, ln0_b, ln1_g, ln1_b, ln2_g, ln2_b, W_out, W_whiten, W_key, W_recep, W_value):
            b, c, h, w = x.shape
            t = x.reshape(b, c, h * w).transpose(0, 2, 1)
            t = _ln(t, ln0_g, ln0_b)
            y1 = _ln(t, ln1_g, ln1_b)
            att = jnp.einsum('btc,oc->bto', jax.nn.sigmoid(y1) * y1, W_out)
            t = t + att
            y2 = _ln(t, ln2_g, ln2_b)
            wht = jnp.einsum('btc,oc->bto', y2, W_whiten)
            k = jnp.square(jax.nn.relu(jnp.einsum('btc,hc->bth', wht, W_key)))
            kv = jnp.einsum('bth,ch->btc', k, W_value)
            r = jax.nn.sigmoid(jnp.einsum('btc,oc->bto', wht, W_recep))
            t = t + r * kv
            return t.transpose(0, 2, 1).reshape(b, c, h, w)
        key = jax.random.key(seed)
        ks = jax.random.split(key, 8)
        b, c, h, w = (4, DIM, 128, 128)
        inp = {'inp_img': jax.random.normal(ks[0], (b, c, h, w), dtype=jnp.float32), 'ln0_g': jnp.ones((c,), jnp.float32), 'ln0_b': jnp.zeros((c,), jnp.float32), 'ln1_g': jnp.ones((c,), jnp.float32), 'ln1_b': jnp.zeros((c,), jnp.float32), 'ln2_g': jnp.ones((c,), jnp.float32), 'ln2_b': jnp.zeros((c,), jnp.float32), 'W_out': jax.random.normal(ks[1], (c, c), jnp.float32) * 0.05, 'W_whiten': jax.random.normal(ks[2], (c, c), jnp.float32) * 0.05, 'W_key': jax.random.normal(ks[3], (HID, c), jnp.float32) * 0.05, 'W_recep': jax.random.normal(ks[4], (c, c), jnp.float32) * 0.05, 'W_value': jax.random.normal(ks[5], (c, HID), jnp.float32) * 0.05}
        return inp
    _L0_conv_all = _L0_conv_setup()
    _L0_conv_in = {k: v for k, v in _L0_conv_all.items() if k in ('ln0_g', 'ln0_b', 'ln1_g', 'ln1_b', 'ln2_g', 'ln2_b', 'W_out', 'W_whiten', 'W_key', 'W_recep', 'W_value', )}
    del _L0_conv_all

    def _L0_ffn_setup():
        import jax, jax.numpy as jnp
        import numpy as np
        B, S, D, E, H, O, K = (512, 2048, 128, 64, 512, 128, 8)
        key = jax.random.key(seed)
        k0, k1, k2, k3 = jax.random.split(key, 4)
        x = jax.random.normal(k0, (B, S, D), dtype=jnp.float32)
        gate_w = jax.random.normal(k1, (E, D), dtype=jnp.float32) * (1.0 / np.sqrt(D))
        gate_b = jnp.zeros((E,), dtype=jnp.float32)
        weight1 = jax.random.uniform(k2, (E, D + 1, H), dtype=jnp.float32, minval=-1.0, maxval=1.0) * (1.0 / np.sqrt(D + 1))
        weight2 = jax.random.uniform(k3, (E, H + 1, O), dtype=jnp.float32, minval=-1.0, maxval=1.0) * (1.0 / np.sqrt(H + 1))
        return {'x': x, 'gate_w': gate_w, 'gate_b': gate_b, 'weight1': weight1, 'weight2': weight2}
    _L0_ffn_all = _L0_ffn_setup()
    _L0_ffn_in = {k: v for k, v in _L0_ffn_all.items() if k in ('gate_w', 'gate_b', 'weight1', 'weight2', )}
    del _L0_ffn_all

    return {
        "x": x,
        "L0_conv_ln0_g": _L0_conv_in["ln0_g"],
        "L0_conv_ln0_b": _L0_conv_in["ln0_b"],
        "L0_conv_ln1_g": _L0_conv_in["ln1_g"],
        "L0_conv_ln1_b": _L0_conv_in["ln1_b"],
        "L0_conv_ln2_g": _L0_conv_in["ln2_g"],
        "L0_conv_ln2_b": _L0_conv_in["ln2_b"],
        "L0_conv_W_out": _L0_conv_in["W_out"],
        "L0_conv_W_whiten": _L0_conv_in["W_whiten"],
        "L0_conv_W_key": _L0_conv_in["W_key"],
        "L0_conv_W_recep": _L0_conv_in["W_recep"],
        "L0_conv_W_value": _L0_conv_in["W_value"],
        "L0_ffn_gate_w": _L0_ffn_in["gate_w"],
        "L0_ffn_gate_b": _L0_ffn_in["gate_b"],
        "L0_ffn_weight1": _L0_ffn_in["weight1"],
        "L0_ffn_weight2": _L0_ffn_in["weight2"],
    }

def reference(x, L0_conv_ln0_g, L0_conv_ln0_b, L0_conv_ln1_g, L0_conv_ln1_b, L0_conv_ln2_g, L0_conv_ln2_b, L0_conv_W_out, L0_conv_W_whiten, L0_conv_W_key, L0_conv_W_recep, L0_conv_W_value, L0_ffn_gate_w, L0_ffn_gate_b, L0_ffn_weight1, L0_ffn_weight2):
    import jax
    import jax.numpy as jnp
    def _L0_conv_ref(inp_img, ln0_g, ln0_b, ln1_g, ln1_b, ln2_g, ln2_b, W_out, W_whiten, W_key, W_recep, W_value):
        import jax, jax.numpy as jnp
        import numpy as np
        DIM = 128
        HID = 4 * DIM
        EPS = 1e-05

        def _ln(x, g, b):
            mu = jnp.mean(x, axis=-1, keepdims=True)
            var = jnp.mean(jnp.square(x - mu), axis=-1, keepdims=True)
            return (x - mu) * jax.lax.rsqrt(var + EPS) * g + b

        def _block(x, ln0_g, ln0_b, ln1_g, ln1_b, ln2_g, ln2_b, W_out, W_whiten, W_key, W_recep, W_value):
            b, c, h, w = x.shape
            t = x.reshape(b, c, h * w).transpose(0, 2, 1)
            t = _ln(t, ln0_g, ln0_b)
            y1 = _ln(t, ln1_g, ln1_b)
            att = jnp.einsum('btc,oc->bto', jax.nn.sigmoid(y1) * y1, W_out)
            t = t + att
            y2 = _ln(t, ln2_g, ln2_b)
            wht = jnp.einsum('btc,oc->bto', y2, W_whiten)
            k = jnp.square(jax.nn.relu(jnp.einsum('btc,hc->bth', wht, W_key)))
            kv = jnp.einsum('bth,ch->btc', k, W_value)
            r = jax.nn.sigmoid(jnp.einsum('btc,oc->bto', wht, W_recep))
            t = t + r * kv
            return t.transpose(0, 2, 1).reshape(b, c, h, w)
        params = (ln0_g, ln0_b, ln1_g, ln1_b, ln2_g, ln2_b, W_out, W_whiten, W_key, W_recep, W_value)
        out1 = _block(inp_img, *params)
        out2 = _block(inp_img.transpose(0, 1, 3, 2), *params).transpose(0, 1, 3, 2)
        return out2 + out1

    def _L0_ffn_ref(x, gate_w, gate_b, weight1, weight2):
        import jax, jax.numpy as jnp
        import numpy as np
        B, S, D, E, H, O, K = (512, 2048, 128, 64, 512, 128, 8)
        Bn, Sn, Dn = x.shape
        logits = jnp.einsum('bsd,ed->bse', x, gate_w) + gate_b
        probs = jax.nn.softmax(logits, axis=1)
        vals, idx = jax.lax.top_k(probs.transpose(0, 2, 1), K)
        topv = vals.transpose(0, 2, 1)
        topi = idx.transpose(0, 2, 1)
        flat_idx = topi.reshape(Bn, K * E)
        gathered = jnp.take_along_axis(x, flat_idx[:, :, None], axis=1)
        gathered = gathered.reshape(Bn, K, E, Dn)
        pooled = jnp.einsum('bked,bke->bed', gathered, topv)
        ones = jnp.ones((E, Bn, 1), dtype=x.dtype)
        h = jnp.concatenate([pooled.transpose(1, 0, 2), ones], axis=-1)
        h = jax.nn.gelu(jnp.einsum('ebd,edh->ebh', h, weight1), approximate=False)
        h = jnp.concatenate([h, ones], axis=-1)
        out = jnp.einsum('ebh,eho->ebo', h, weight2)
        out = out.transpose(1, 0, 2)
        weighted = jnp.einsum('beo,bke->bkeo', out, topv).reshape(Bn, K * E, O)
        outputs = jnp.zeros((Bn, Sn, O), dtype=x.dtype)
        outputs = outputs.at[jnp.arange(Bn)[:, None], flat_idx].add(weighted)
        return outputs

    def _gn(v, G=32, eps=1e-5):
        B_, C_, H_, W_ = v.shape
        g = v.reshape(B_, G, C_ // G, H_, W_)
        m = jnp.mean(g, axis=(2, 3, 4), keepdims=True)
        s = jnp.var(g, axis=(2, 3, 4), keepdims=True)
        return ((g - m) / jnp.sqrt(s + eps)).reshape(v.shape)

    def _ln_c(v, eps=1e-6):
        m = jnp.mean(v, axis=1, keepdims=True)
        s = jnp.var(v, axis=1, keepdims=True)
        return (v - m) / jnp.sqrt(s + eps)

    def _ln_t(v, eps=1e-5):
        m = jnp.mean(v, axis=-1, keepdims=True)
        s = jnp.var(v, axis=-1, keepdims=True)
        return (v - m) / jnp.sqrt(s + eps)

    def _to_tokens(v):
        B_, C_, H_, W_ = v.shape
        return v.reshape(B_, C_, H_ * W_).transpose(0, 2, 1)
    def _from_tokens(t, like):
        B_, C_, H_, W_ = like.shape
        return t.transpose(0, 2, 1).reshape(B_, C_, H_, W_)

    x = x + _L0_conv_ref(_ln_c(x), L0_conv_ln0_g, L0_conv_ln0_b, L0_conv_ln1_g, L0_conv_ln1_b, L0_conv_ln2_g, L0_conv_ln2_b, L0_conv_W_out, L0_conv_W_whiten, L0_conv_W_key, L0_conv_W_recep, L0_conv_W_value)
    t = _to_tokens(x)
    t = t + _L0_ffn_ref(_ln_t(t), L0_ffn_gate_w, L0_ffn_gate_b, L0_ffn_weight1, L0_ffn_weight2)
    x = _from_tokens(t, x)
    return x


_drawn_inputs = setup_inputs


def setup_inputs(seed=0):
    import zlib

    import numpy as np

    out = dict(_drawn_inputs(seed))
    spreads = {'L0_conv_ln0_g': (1.0, 0.2),
     'L0_conv_ln0_b': (0.0, 0.1),
     'L0_conv_ln1_g': (1.0, 0.2),
     'L0_conv_ln1_b': (0.0, 0.401),
     'L0_conv_ln2_g': (1.0, 0.6),
     'L0_conv_ln2_b': (0.0, 0.8),
     'L0_ffn_gate_b': (0.0, 0.1)}
    factors = {'L0_conv_W_recep': 6.896,
     'L0_ffn_gate_w': 8.0,
     'L0_ffn_weight1': 8.0,
     'L0_ffn_weight2': 8.0}
    for name, (base, spread) in spreads.items():
        noise = np.random.default_rng([zlib.crc32(name.encode()), seed]).standard_normal(out[name].shape)
        drawn = base * np.exp(spread * noise) if base else spread * noise
        out[name] = jnp.asarray(drawn.astype(out[name].dtype))
    for name, factor in factors.items():
        out[name] = (out[name] * factor).astype(out[name].dtype)
    return out
```

```python
from contextlib import ExitStack

import concourse.bass as bass
from concourse import mybir

F32 = mybir.dt.float32
U32 = mybir.dt.uint32
ALU = mybir.AluOpType
ACT = mybir.ActivationFunctionType
AX = mybir.AxisListType

P = 128
BATCH, TOKENS = 4, 128 * 128
HALF = 512
UNIT = 2 * HALF
GROUPS = UNIT // P
PAIR_UNITS = TOKENS // HALF
UNITS = BATCH // 2 * PAIR_UNITS
HID = 512
CHUNKS = HID // P
EXPERTS, TOPK, FFN = 64, 8, 512
FC = FFN // P
FG = 4
LOTS = EXPERTS // FG
LOT = FG * (FFN + FC * P)
RING = 2
CAND = PAIR_UNITS * TOPK

_at = 0
COL = {}
for _name, _n in (("g0", P), ("b0", P), ("w_out", P), ("w_whiten", P), ("w_key", HID), ("w_recep", P),
                  ("w_value", HID), ("gate_w", EXPERTS), ("g1", 1), ("b1", 1), ("g2", 1), ("b2", 1),
                  ("gate_b", 1), ("ffn_b1", EXPERTS * FC), ("ffn_b2", EXPERTS)):
    COL[_name] = (_at, _at + _n)
    _at += _n
COLS = _at

LN = {0: (1.0 + 1e-5, 1e-11), 1: (1.0, 1e-5), 2: (1.0, 1e-5), 3: (1.0, 1e-5)}
LN_STEPS = 8

SQUARES = {0: "dve", 1: "act", 2: "act", 3: "act"}
SQ_N = {e: sum(v == e for v in SQUARES.values()) for e in ("dve", "act", "pool")}
SQ_K = {c: sum(SQUARES[d] == SQUARES[c] for d in range(c + 1)) for c in SQUARES}

FIRST_LOOP, LAST_LOOP = 3, 60


def metaformer_kernel(nc, x, cst, wff, out):
    ctx = ExitStack()
    with ctx:
        def sb(name, shape, dt=F32):
            return ctx.enter_context(nc.sbuf_tensor(name, shape, dt))

        def sem(name):
            return ctx.enter_context(nc.semaphore(name))

        C = sb("constants", [P, COLS])
        ident = sb("ident", [P, P])
        w_out = sb("w_out_half", [P, P])
        w_key = sb("w_key_folded", [P, HID])
        w_recep = sb("w_recep_folded", [P, P])
        bias_kr = sb("bias_key_recep", [P, CHUNKS + 1])
        g_half = sb("minus_half", [P, 2 * TOPK])
        g_quarter = sb("quarter_scale", [P, 2, 2 * TOPK])

        def col(name):
            return C[:, COL[name][0]:COL[name][1]]

        xt = sb("x_tok", [P, 2, GROUPS, P])
        z0 = sb("z0_tok", [P, GROUPS, P])
        t0 = sb("t0_tok", [P, 2, GROUPS, P])
        z1 = sb("z1_tok", [P, GROUPS, P])
        y1 = sb("y1_chan", [P, UNIT])
        sl = sb("silu_chan", [P, UNIT])
        t1 = sb("t1_tok", [P, GROUPS, P])
        res = sb("residual_tok", [P, 2, GROUPS, P])
        z2 = sb("z2_tok", [P, GROUPS, P])
        y2 = sb("y2_chan", [P, 2, UNIT])
        gate_r = sb("recep_tanh_chan", [P, UNIT])
        hid = sb("hidden", [P, CHUNKS, UNIT])
        rk = sb("rkv_chan", [P, UNIT])
        x1 = sb("x1_tok", [P, 2, GROUPS, P])
        z3 = sb("z3_tok", [P, GROUPS, P])
        tn = sb("tn_chan", [P, UNIT])
        lg = sb("logits", [P, HALF])
        ex = sb("exp_scratch", [P, HALF])
        st = [sb(f"stats{n}", [P, GROUPS, 6]) for n in range(4)]
        sm = [sb(f"sums{n}", [P, GROUPS, 2]) for n in range(4)]
        df = [sb(f"diffs{n}", [P, GROUPS]) for n in range(4)]
        va = [sb(f"var{n}", [P, GROUPS]) for n in range(4)]
        mean = [sb(f"mean{n}", [P, GROUPS]) for n in range(4)]
        rstd = [sb(f"rstd{n}", [P, GROUPS]) for n in range(4)]

        mx = sb("unit_max8", [P, 2, TOPK])
        mi = sb("unit_index8", [P, 2, TOPK], U32)
        neg = sb("unit_neg_max", [P, 2])
        cval = sb("cand_values", [P, UNITS * TOPK])
        cidx = sb("cand_index", [P, UNITS * TOPK])
        csum = sb("unit_exp_sums", [P, UNITS])

        ring = sb("expert_weights", [P, RING, LOT])

        iota_i = sb("iota_int", [P, 2, CAND], mybir.dt.int32)
        iota_f = sb("iota_pos_tile", [P, 2, CAND])
        half_bit = sb("half_bit", [P, 2 * TOPK], U32)
        v8 = sb("top_values", [P, 2, TOPK])
        pos = sb("top_pos", [P, 2, TOPK], U32)
        posf = sb("top_pos_f", [P, 2, TOPK])
        seq = sb("top_token", [P, 2 * TOPK])
        rows_t = sb("row_parts", [P, 4, 2 * TOPK], U32)
        rows = sb("rows", [P, 2 * TOPK], U32)
        rowsf = sb("rows_f", [P, 2 * TOPK])
        neg_m = sb("neg_top", [P, 2])
        e_max = sb("exp_unit_max", [P, 2, PAIR_UNITS])
        den = sb("denominator", [P, 2])
        rden = sb("rdenominator", [P, 2])
        prob = sb("probs", [P, 2, TOPK])
        g_st = sb("g_stats", [P, 2 * TOPK, 6])
        g_sm = sb("g_sums", [P, 2 * TOPK, 2])
        g_df = sb("g_diffs", [P, 2 * TOPK])
        g_va = sb("g_var", [P, 2 * TOPK])
        g_mean = sb("g_mean", [P, 2 * TOPK])
        g_rstd = sb("g_rstd", [P, 2 * TOPK])
        pooled = sb("pooled", [P, 2, 2, P])
        pooled_t = sb("pooled_chan", [P, BATCH, EXPERTS])
        hpre = sb("expert_pre", [P, 2, FG * FC * BATCH])
        hact = sb("expert_hidden", [P, 2, FG * FC * BATCH])
        ffn_t = sb("expert_out_chan", [P, BATCH, EXPERTS])
        ffn_o = sb("expert_out", [P, 2, P])
        junk = ex[:, 0:CAND]
        picked = hid[:, 0:2, :].rearrange("p a (k c) -> p (a k) c", c=P)
        normed = hid[:, 2:4, :].rearrange("p a (k c) -> p (a k) c", c=P)
        row_b = xt[:, :, :, :].rearrange("p a g c -> p (a g) c")
        row_all = t0[:, :, :, :].rearrange("p a g c -> p a (g c)")
        share = res[:, :, :, :].rearrange("p a g c -> p a (g c)")
        part = y2[:, :, :]
        final = x1[:, :, :, :].rearrange("p a g c -> p (a g) c")

        kps = [ctx.enter_context(nc.psum_tensor(f"key{n}", [P, UNIT], F32)) for n in range(2)]
        kv = ctx.enter_context(nc.psum_tensor("kv", [P, UNIT], F32))
        ms = ctx.enter_context(nc.psum_tensor("misc", [P, UNIT], F32))

        cst_loaded = sem("cst_loaded")
        x_loaded = [sem("x_loaded0"), sem("x_loaded1")]
        x1_stored = [sem("x1_stored0"), sem("x1_stored1")]
        lot_loaded = [sem(f"lot_loaded{n}") for n in range(RING)]
        pool_const = sem("pool_const")
        fold_mm, fold_raw, fold_bias, fold_ready = sem("fold_mm"), sem("fold_raw"), sem("fold_bias"), sem("fold_ready")
        iota_ready = sem("iota_ready")
        stats_ready = [sem(f"stats_ready{n}") for n in range(4)]
        ln_steps = [sem(f"ln_steps{n}") for n in range(4)]
        z_ready = [sem(f"z_ready{n}") for n in range(4)]
        t0_steps = sem("t0_steps")
        z1_turned, y1_ready, tanh_ready, silu_ready = sem("z1_turned"), sem("y1_ready"), sem("tanh_ready"), sem("silu_ready")
        att_done, t1_ready, res_ready = sem("att_done"), sem("t1_ready"), sem("res_ready")
        z2_turned, y2_ready = sem("z2_turned"), sem("y2_ready")
        recep_done, recep_ready = sem("recep_done"), sem("recep_ready")
        key_done, relu_done, value_done = sem("key_done"), sem("relu_done"), sem("value_done")
        sq_done = {e: sem(f"squares_{e}") for e in ("dve", "act", "pool")}
        rk_ready, rk_turned, x1_ready = sem("rk_ready"), sem("rk_turned"), sem("x1_ready")
        z3_turned, tn_ready = sem("z3_turned"), sem("tn_ready")
        gate_done, lg_ready = sem("gate_done"), sem("lg_ready")
        max_ready, index_ready, neg_ready, exp_ready, cand_kept = (
            sem("max_ready"), sem("index_ready"), sem("neg_ready"), sem("exp_ready"), sem("cand_kept"))
        pick, negm_ready, emax_ready, den_ready = sem("pick"), sem("negm_ready"), sem("emax_ready"), sem("den_ready")
        rows_ready, gathered, probs_ready = sem("rows_ready"), sem("gathered"), sem("probs_ready")
        g_stats_ready, g_ln, pooling, pool_turned = sem("g_stats_ready"), sem("g_ln"), sem("pooling"), sem("pool_turned")
        pooled_ready, up_done, pre_ready, gelu_ready, down_done = (
            sem("pooled_ready"), sem("up_done"), sem("pre_ready"), sem("gelu_ready"), sem("down_done"))
        rowb_ready, row_turned, row_copied, sharing = sem("rowb_ready"), sem("row_turned"), sem("row_copied"), sem("sharing")
        ffnt_ready, ffn_turned, ffno_ready, added_done, final_ready, scattered = (
            sem("ffnt_ready"), sem("ffn_turned"), sem("ffno_ready"), sem("added_done"), sem("final_ready"), sem("scattered"))

        def at(u, d):
            return (u[0] + d, u[1])

        def num(u):
            return u[0] if u[1] is None else u[1] * 2 + u[0]

        def real(u):
            return u[1] is not None or 0 <= u[0] < UNITS

        def wait(eng, s, u, per=1, k=None):
            v = per * u[0] + (per if k is None else k)
            if u[1] is not None:
                eng.wait_ge(s, u[1] * (2 * per) + v)
            elif v > 0:
                eng.wait_ge(s, v)

        def wait_dma(eng, s, u):
            v = 16 * (u[0] // 2 + 1)
            if u[1] is not None:
                eng.wait_ge(s, u[1] * 16 + v)
            elif v > 0:
                eng.wait_ge(s, v)

        def run_steps(eng, step):
            for i in range(-2, FIRST_LOOP):
                step((i, None))
            with eng.Fori(0, (LAST_LOOP - FIRST_LOOP + 1) // 2) as j:
                step((FIRST_LOOP, j))
                step((FIRST_LOOP + 1, j))
            for i in range(LAST_LOOP + 1, UNITS + 2):
                step((i, None))

        block = ctx.enter_context(nc.Block())

        @block.sync
        def _(sp):
            def load_x(u):
                if real(u):
                    wait(sp, res_ready, at(u, -2))
                    sp.dma_start(xt[:, u[0] % 2, :, :].rearrange("p g c -> p (g c)"),
                                 x[bass.ds(num(u), 1), :, :].rearrange("a p n -> (a p) n")
                                 ).then_inc(x_loaded[u[0] % 2], 16)

            def step(i):
                b = at(i, -1)
                if real(b):
                    wait(sp, x1_ready, b)
                    sp.dma_start(out[bass.ds(num(b), 1), :, :].rearrange("a p n -> (a p) n"),
                                 x1[:, b[0] % 2, :, :].rearrange("p g c -> p (g c)")
                                 ).then_inc(x1_stored[b[0] % 2], 16)
                load_x(at(i, 3))

            sp.dma_start(C[:, :], cst[:, :]).then_inc(cst_loaded, 16)
            load_x((0, None))
            for n in range(RING):
                sp.dma_start(ring[:, n, :], wff[n, :, :]).then_inc(lot_loaded[n], 16)
            run_steps(sp, step)
            for g in range(RING, LOTS):
                sp.wait_ge(down_done, g - RING + 1)
                sp.dma_start(ring[:, g % RING, :], wff[g, :, :]).then_inc(lot_loaded[g % RING], 16)

        def ln_on_pool(pool, s, base, stat, sums, diff, var, mu, rs, exponent, quarter, scale, eps):
            tt, ts = nc.gpsimd.tensor_tensor, nc.gpsimd.tensor_scalar
            tt(out=sums, in0=stat[:, :, 1:3], in1=stat[:, :, 4:6], op=ALU.add).then_inc(s, 1)
            tt(out=diff, in0=stat[:, :, 1], in1=stat[:, :, 4], op=ALU.subtract).then_inc(s, 1)
            base(2)
            tt(out=diff, in0=diff, in1=diff, op=ALU.mult).then_inc(s, 1)
            ts(mu, sums[:, :, 0], 0.5, None, ALU.mult).then_inc(s, 1)
            ts(var, sums[:, :, 1], scale / P, eps, ALU.mult, ALU.add).then_inc(s, 1)
            base(3)
            tt(out=diff, in0=diff, in1=quarter, op=ALU.mult).then_inc(s, 1)
            base(6)
            tt(out=var, in0=var, in1=diff, op=ALU.add).then_inc(s, 1)
            base(7)
            tt(out=rs, in0=var, in1=exponent, op=ALU.pow).then_inc(s, 1)

        @block.gpsimd
        def _(pool):
            def ln(n, u):
                wait(pool, stats_ready[n], u)
                wait(pool, z_ready[n], at(u, -1))
                ln_on_pool(pool, ln_steps[n], lambda k: wait(pool, ln_steps[n], u, LN_STEPS, k),
                           st[n][:, :, :], sm[n][:, :, :], df[n][:, :], va[n][:, :], mean[n][:, :], rstd[n][:, :],
                           g_half[:, 0:GROUPS], g_quarter[:, min(n, 1), 0:GROUPS], *LN[n])

            def step(i):
                a, f, b, c = at(i, 2), at(i, 1), at(i, -1), at(i, -2)
                if real(a):
                    ln(0, a)
                if real(c):
                    wait(pool, index_ready, c)
                    v = num(c) * TOPK
                    nc.gpsimd.tensor_copy(cval[:, bass.ds(v, TOPK)], mx[:, c[0] % 2, :]).then_inc(cand_kept, 1)
                    nc.gpsimd.tensor_copy(cidx[:, bass.ds(v, TOPK)], mi[:, c[0] % 2, :]).then_inc(cand_kept, 1)
                if real(a):
                    wait(pool, z_ready[0], a)
                    wait(pool, t1_ready, at(a, -2))
                    nc.gpsimd.tensor_tensor(out=z0[:, :, :], in0=z0[:, :, :],
                                            in1=col("g0")[:, None, :].to_broadcast([P, GROUPS, P]),
                                            op=ALU.mult).then_inc(t0_steps, 1)
                    wait(pool, t0_steps, a, 2, 1)
                    nc.gpsimd.tensor_tensor(out=t0[:, a[0] % 2, :, :], in0=z0[:, :, :],
                                            in1=col("b0")[:, None, :].to_broadcast([P, GROUPS, P]),
                                            op=ALU.add).then_inc(t0_steps, 1)
                if real(b):
                    ln(3, b)
                if real(i):
                    for ch in range(CHUNKS):
                        if SQUARES[ch] == "pool":
                            wait(pool, relu_done, i, CHUNKS, ch + 1)
                            nc.gpsimd.tensor_tensor(out=hid[:, ch, :], in0=hid[:, ch, :], in1=hid[:, ch, :],
                                                    op=ALU.mult).then_inc(sq_done["pool"], 1)
                if real(f):
                    ln(2, f)
                if real(a):
                    ln(1, a)

            nc.gpsimd.memset(ident[:, :], 0.0).then_inc(pool_const, 1)
            nc.gpsimd.memset(g_half[:, :], -0.5).then_inc(pool_const, 1)
            for n in range(2):
                nc.gpsimd.memset(g_quarter[:, n, :], LN[n][0] / 4).then_inc(pool_const, 1)
            pool.wait_ge(pool_const, 4)
            nc.gpsimd.affine_select(out=ident[:, :], in_=ident[:, :], compare_op=ALU.not_equal, fill=1.0, base=0,
                                    pattern=[[-1, P]], channel_multiplier=1).then_inc(pool_const, 1)
            nc.gpsimd.iota(iota_i[:, 0, :], pattern=[[1, CAND]], base=0, channel_multiplier=0).then_inc(pool_const, 1)
            nc.gpsimd.iota(iota_i[:, 1, :], pattern=[[HALF, PAIR_UNITS], [0, TOPK]], base=0,
                           channel_multiplier=0).then_inc(pool_const, 1)
            nc.gpsimd.iota(half_bit[:, :], pattern=[[0, 2 * TOPK]], base=0, channel_multiplier=1).then_inc(pool_const, 1)
            pool.wait_ge(pool_const, 8)
            nc.gpsimd.tensor_copy(iota_f[:, :, :], iota_i[:, :, :]).then_inc(iota_ready, 1)
            pool.wait_ge(cst_loaded, 16)
            run_steps(pool, step)

            for par in range(2):
                pool.wait_ge(x1_stored[par], 16 * (UNITS // 2))
            for q in range(2):
                pool.wait_ge(rows_ready, q + 1)
                for k in range(TOPK):
                    nc.gpsimd.indirect_dma_start(
                        out=picked[:, q * TOPK + k, :], out_offset=None, in_=out.rearrange("u p (g c) -> (u p g) c", c=P),
                        in_offset=bass.IndirectOffsetOnAxis(ap=rows[:, q * TOPK + k:q * TOPK + k + 1], axis=0)
                    ).then_inc(gathered, 16)
            pool.wait_ge(g_stats_ready, 1)
            ln_on_pool(pool, g_ln, lambda k: pool.wait_ge(g_ln, k), g_st[:, :, :], g_sm[:, :, :], g_df[:, :],
                       g_va[:, :], g_mean[:, :], g_rstd[:, :], g_half[:, :], g_quarter[:, 1, :], *LN[3])
            for q in range(2):
                pool.wait_ge(final_ready, q + 1)
                for k in range(TOPK):
                    if q or k:
                        pool.wait_ge(scattered, 16 * (q * TOPK + k))
                    nc.gpsimd.indirect_dma_start(
                        out=out.rearrange("u p (g c) -> (u p g) c", c=P),
                        out_offset=bass.IndirectOffsetOnAxis(ap=rows[:, q * TOPK + k:q * TOPK + k + 1], axis=0),
                        in_=final[:, q * TOPK + k, :], in_offset=None).then_inc(scattered, 16)
            pool.wait_ge(scattered, 16 * 2 * TOPK)

        @block.scalar
        def _(act):
            def relu(i, ch):
                wait(act, key_done, i, CHUNKS, ch + 1)
                wait(act, value_done, at(i, -1), CHUNKS, ch + 1)
                nc.scalar.activation(hid[:, ch, :], kps[ch % 2][:, :], ACT.Relu,
                                     bias=bias_kr[:, ch:ch + 1]).then_inc(relu_done, 1)

            def square(i, ch):
                if SQUARES[ch] == "act":
                    wait(act, relu_done, i, CHUNKS, ch + 1)
                    nc.scalar.activation(hid[:, ch, :], hid[:, ch, :], ACT.Square).then_inc(sq_done["act"], 1)

            def step(i):
                f, b, c = at(i, 1), at(i, -1), at(i, -2)
                if real(i):
                    relu(i, 0)
                if real(f):
                    wait(act, z1_turned, f)
                    wait(act, silu_ready, at(f, -1))
                    nc.scalar.activation(y1[:, :], ms[:, :], ACT.Identity, bias=col("b1"),
                                         scale=col("g1")).then_inc(y1_ready, 1)
                    wait(act, y1_ready, f)
                    wait(act, att_done, at(f, -1))
                    nc.scalar.activation(sl[:, :], y1[:, :], ACT.Tanh, scale=0.5).then_inc(tanh_ready, 1)
                if real(i):
                    square(i, 0)
                    relu(i, 1)
                    wait(act, recep_done, i)
                    wait(act, rk_ready, at(i, -1))
                    nc.scalar.activation(gate_r[:, :], ms[:, :], ACT.Tanh, bias=bias_kr[:, CHUNKS:CHUNKS + 1],
                                         scale=0.5).then_inc(recep_ready, 1)
                    square(i, 1)
                    relu(i, 2)
                    square(i, 2)
                if real(c):
                    wait(act, neg_ready, c)
                    wait(act, exp_ready, at(c, -1))
                    nc.scalar.activation(ex[:, :], lg[:, :], ACT.Exp, bias=neg[:, c[0] % 2:c[0] % 2 + 1],
                                         accum_out=csum[:, bass.ds(num(c), 1)]).then_inc(exp_ready, 1)
                if real(b):
                    wait(act, z3_turned, b)
                    wait(act, gate_done, at(b, -1))
                    nc.scalar.activation(tn[:, :], ms[:, :], ACT.Copy).then_inc(tn_ready, 1)
                if real(i):
                    relu(i, 3)
                    square(i, 3)
                if real(f):
                    wait(act, z2_turned, f)
                    wait(act, key_done, at(f, -2), CHUNKS)
                    nc.scalar.activation(y2[:, f[0] % 2, :], ms[:, :], ACT.Copy).then_inc(y2_ready, 1)
                if real(b):
                    wait(act, gate_done, b)
                    wait(act, index_ready, at(b, -1))
                    wait(act, exp_ready, at(b, -1))
                    nc.scalar.activation(lg[:, :], ms[:, 0:HALF], ACT.Identity,
                                         bias=col("gate_b")).then_inc(lg_ready, 1)

            act.wait_ge(cst_loaded, 16)
            act.wait_ge(fold_mm, 1)
            nc.scalar.activation(hid[:, 0, 0:HID], kps[0][:, 0:HID], ACT.Copy).then_inc(fold_raw, 1)
            nc.scalar.activation(hid[:, 1, 0:P], kps[1][:, 0:P], ACT.Copy).then_inc(fold_raw, 1)
            nc.scalar.activation(w_key[:, :], kps[0][:, 0:HID], ACT.Identity, scale=col("g2")).then_inc(fold_ready, 1)
            nc.scalar.activation(w_recep[:, :], kps[1][:, 0:P], ACT.Identity, scale=col("g2")).then_inc(fold_ready, 1)
            nc.scalar.activation(w_out[:, :], col("w_out"), ACT.Copy, scale=0.5).then_inc(fold_ready, 1)
            act.wait_ge(fold_bias, 1)
            nc.scalar.activation(bias_kr[:, 0:CHUNKS], ms[:, 0:CHUNKS], ACT.Copy).then_inc(fold_ready, 1)
            nc.scalar.activation(bias_kr[:, CHUNKS:CHUNKS + 1], ms[:, CHUNKS:CHUNKS + 1], ACT.Copy,
                                 scale=0.5).then_inc(fold_ready, 1)
            act.wait_ge(fold_ready, 5)
            run_steps(act, step)

            act.wait_ge(cand_kept, 2 * UNITS)
            for q in range(2):
                act.wait_ge(negm_ready, q + 1)
                nc.scalar.activation(
                    e_max[:, q, :], cval[:, q * CAND:(q + 1) * CAND].rearrange("p (u k) -> p u k", k=TOPK)[:, :, 0],
                    ACT.Exp, bias=neg_m[:, q:q + 1]).then_inc(emax_ready, 1)
                nc.scalar.activation(prob[:, q, :], v8[:, q, :], ACT.Exp, bias=neg_m[:, q:q + 1]).then_inc(emax_ready, 1)
            for q in range(2):
                act.wait_ge(row_turned, q + 1)
                nc.scalar.activation(row_all[:, q, :], kps[q][:, :], ACT.Copy).then_inc(row_copied, 1)
            for g in range(LOTS):
                act.wait_ge(pre_ready, g + 1)
                if g >= 2:
                    act.wait_ge(down_done, g - 1)
                nc.scalar.activation(hact[:, g % 2, :], hpre[:, g % 2, :], ACT.Gelu).then_inc(gelu_ready, 1)

        @block.vector
        def _(dve):
            ts, tt, stt = nc.vector.tensor_scalar, nc.vector.tensor_tensor, nc.vector.scalar_tensor_tensor

            def stats(n, src, u):
                for g in range(GROUPS):
                    last = nc.vector.bn_stats(st[n][:, g, :], src[:, g, :])
                last.then_inc(stats_ready[n], 1)

            def normalise(n, dst, src, u):
                wait(dve, ln_steps[n], u, LN_STEPS)
                for g in range(GROUPS):
                    last = ts(dst[:, g, :], src[:, g, :], mean[n][:, g:g + 1], rstd[n][:, g:g + 1],
                              ALU.subtract, ALU.mult)
                last.then_inc(z_ready[n], 1)

            def square(i, ch):
                if SQUARES[ch] == "dve":
                    wait(dve, relu_done, i, CHUNKS, ch + 1)
                    tt(hid[:, ch, :], hid[:, ch, :], hid[:, ch, :], ALU.mult).then_inc(sq_done["dve"], 1)

            def flat(t):
                return t.rearrange("p g c -> p (g c)")

            def step(i):
                a, f, b, c = at(i, 2), at(i, 1), at(i, -1), at(i, -2)
                if real(b):
                    wait(dve, value_done, b, CHUNKS)
                    wait(dve, recep_ready, b)
                    wait(dve, rk_turned, at(b, -1))
                    stt(out=rk[:, :], in0=gate_r[:, :], scalar=1.0, in1=kv[:, :], op0=ALU.add,
                        op1=ALU.mult).then_inc(rk_ready, 1)
                if real(c):
                    wait(dve, cand_kept, at(c, -2), 2)
                    wait(dve, exp_ready, at(c, -2))
                    wait(dve, lg_ready, c)
                if real(a):
                    wait_dma(dve, x_loaded[a[0] % 2], a)
                    stats(0, xt[:, a[0] % 2, :, :], a)
                if real(c):
                    nc.vector.max(mx[:, c[0] % 2, :], lg[:, :]).then_inc(max_ready, 1)
                    wait(dve, max_ready, c)
                    ts(neg[:, c[0] % 2:c[0] % 2 + 1], mx[:, c[0] % 2, 0:1], -1.0, None, ALU.mult).then_inc(neg_ready, 1)
                    nc.vector.max_index(mi[:, c[0] % 2, :], mx[:, c[0] % 2, :], lg[:, :]).then_inc(index_ready, 1)
                if real(i):
                    square(i, 0)
                if real(f):
                    wait(dve, tanh_ready, f)
                    stt(out=sl[:, :], in0=sl[:, :], scalar=1.0, in1=y1[:, :], op0=ALU.add,
                        op1=ALU.mult).then_inc(silu_ready, 1)
                if real(a):
                    wait(dve, t0_steps, at(a, -1), 2)
                    normalise(0, z0, xt[:, a[0] % 2, :, :], a)
                if real(b):
                    wait(dve, rk_turned, b)
                    wait_dma(dve, x1_stored[b[0] % 2], at(b, -2))
                    tt(flat(x1[:, b[0] % 2, :, :]), flat(res[:, b[0] % 2, :, :]), ms[:, :],
                       ALU.add).then_inc(x1_ready, 1)
                    wait(dve, x1_ready, b)
                    stats(3, x1[:, b[0] % 2, :, :], b)
                if real(i):
                    square(i, 1)
                if real(b):
                    wait(dve, z3_turned, at(b, -1))
                    normalise(3, z3, x1[:, b[0] % 2, :, :], b)
                if real(f):
                    wait(dve, att_done, f)
                    wait(dve, res_ready, at(f, -1))
                    tt(flat(t1[:, :, :]), flat(t0[:, f[0] % 2, :, :]), ms[:, :], ALU.add).then_inc(t1_ready, 1)
                    wait(dve, t1_ready, f)
                    stats(2, t1, f)
                    stt(out=flat(res[:, f[0] % 2, :, :]), in0=flat(t1[:, :, :]), scalar=2.0,
                        in1=flat(xt[:, f[0] % 2, :, :]), op0=ALU.mult, op1=ALU.add).then_inc(res_ready, 1)
                if real(a):
                    wait(dve, t0_steps, a, 2)
                    stats(1, t0[:, a[0] % 2, :, :], a)
                if real(i):
                    square(i, 2)
                if real(f):
                    wait(dve, z2_turned, at(f, -1))
                    normalise(2, z2, t1, f)
                if real(a):
                    wait(dve, z1_turned, at(a, -1))
                    normalise(1, z1, t0[:, a[0] % 2, :, :], a)
                if real(i):
                    square(i, 3)

            run_steps(dve, step)

            count = [0]

            def then(ins):
                count[0] += 1
                ins.then_inc(pick, 1)
                dve.wait_ge(pick, count[0])

            dve.wait_ge(cand_kept, 2 * UNITS)
            dve.wait_ge(exp_ready, UNITS)
            dve.wait_ge(iota_ready, 1)
            then(ts(half_bit[:, :], half_bit[:, :], 6, 2, ALU.logical_shift_right, ALU.logical_shift_left))
            for q in range(2):
                vals, idxs = cval[:, q * CAND:(q + 1) * CAND], cidx[:, q * CAND:(q + 1) * CAND]
                then(nc.vector.max(v8[:, q, :], vals))
                ts(neg_m[:, q:q + 1], v8[:, q, 0:1], -1.0, None, ALU.mult).then_inc(negm_ready, 1)
                then(nc.vector.max_index(pos[:, q, :], v8[:, q, :], vals))
                then(nc.vector.tensor_copy(posf[:, q, :], pos[:, q, :]))
                then(tt(idxs, idxs, iota_f[:, 1, :], ALU.add))
                for k in range(TOPK):
                    then(stt(out=junk, in0=iota_f[:, 0, :], scalar=posf[:, q, k:k + 1], in1=idxs, op0=ALU.is_equal,
                             op1=ALU.mult, accum_out=seq[:, q * TOPK + k:q * TOPK + k + 1]))
                w = slice(q * TOPK, (q + 1) * TOPK)
                r = rows_t[:, :, w]
                then(nc.vector.tensor_copy(r[:, 0, :], seq[:, w]))
                then(ts(r[:, 1, :], r[:, 0, :], 9, 10, ALU.logical_shift_right, ALU.logical_shift_left))
                then(ts(r[:, 2, :], r[:, 0, :], P - 1, 3, ALU.bitwise_and, ALU.logical_shift_left))
                then(ts(r[:, 3, :], r[:, 0, :], 7, 3, ALU.logical_shift_right, ALU.bitwise_and))
                then(tt(r[:, 1, :], r[:, 1, :], r[:, 2, :], ALU.bitwise_or))
                then(tt(r[:, 3, :], r[:, 3, :], half_bit[:, w], ALU.bitwise_or))
                then(tt(r[:, 1, :], r[:, 1, :], r[:, 3, :], ALU.bitwise_or))
                ts(rows[:, w], r[:, 1, :], q * 2 * TOKENS, None, ALU.bitwise_or).then_inc(rows_ready, 1)
            dve.wait_ge(rows_ready, 2)
            then(nc.vector.tensor_copy(rowsf[:, :], rows[:, :]))
            for q in range(2):
                dve.wait_ge(emax_ready, 2 * q + 2)
                then(stt(out=junk[:, 0:PAIR_UNITS], in0=e_max[:, q, :], scalar=1.0,
                         in1=csum[:, q * PAIR_UNITS:(q + 1) * PAIR_UNITS], op0=ALU.mult, op1=ALU.mult,
                         accum_out=den[:, q:q + 1]))
                then(nc.vector.reciprocal(rden[:, q:q + 1], den[:, q:q + 1]))
                then(ts(prob[:, q, :], prob[:, q, :], rden[:, q:q + 1], None, ALU.mult))
            for n in range(2 * TOPK):
                last = nc.vector.tensor_copy(row_b[:, n, :], rowsf[:, n:n + 1].to_broadcast([P, P]))
            last.then_inc(rowb_ready, 1)
            dve.wait_ge(gathered, 16 * 2 * TOPK)
            for n in range(2 * TOPK):
                last = nc.vector.bn_stats(g_st[:, n, :], picked[:, n, :])
            last.then_inc(g_stats_ready, 1)
            dve.wait_ge(g_ln, LN_STEPS)
            for n in range(2 * TOPK):
                last = ts(normed[:, n, :], picked[:, n, :], g_mean[:, n:n + 1], g_rstd[:, n:n + 1],
                          ALU.subtract, ALU.mult)
            then(last)
            for k in range(TOPK):
                for q in range(2):
                    if k == 0:
                        last = ts(pooled[:, q, 0, :], normed[:, q * TOPK, :], prob[:, q, 0:1], None, ALU.mult)
                    else:
                        last = stt(out=pooled[:, q, k % 2, :], in0=normed[:, q * TOPK + k, :],
                                   scalar=prob[:, q, k:k + 1], in1=pooled[:, q, (k - 1) % 2, :],
                                   op0=ALU.mult, op1=ALU.add)
                then(last)
            nc.vector.tensor_copy(pooled[:, :, 0, :], pooled[:, :, 1, :]).then_inc(pooling, 1)
            dve.wait_ge(pool_turned, 1)
            nc.vector.tensor_copy(pooled_t[:, :, :].rearrange("p b e -> p (b e)"), ms[:, 0:2 * P]).then_inc(pooled_ready, 1)

            def share_of(q):
                dve.wait_ge(row_copied, q + 1)
                for k in range(TOPK):
                    dst = share[:, q, :] if k == 0 else part[:, k % 2, :]
                    then(ts(dst, row_all[:, q, :], rowsf[:, q * TOPK + k:q * TOPK + k + 1], prob[:, q, k:k + 1],
                            ALU.is_equal, ALU.mult))
                    if k:
                        then(tt(share[:, q, :], share[:, q, :], part[:, k % 2, :], ALU.add))
                nc.vector.tensor_copy(den[:, q:q + 1], rden[:, q:q + 1]).then_inc(sharing, 1)

            b1v = col("ffn_b1").rearrange("p (e f) -> p e f", f=FC)
            for g in range(LOTS):
                dve.wait_ge(up_done, g + 1)
                if g >= 2:
                    dve.wait_ge(gelu_ready, g - 1)
                w = FG * FC * BATCH
                tt(hpre[:, g % 2, :].rearrange("p (a b) -> p a b", b=BATCH),
                   kv[:, 512 * (g % 2):512 * (g % 2) + w].rearrange("p (a b) -> p a b", b=BATCH),
                   col("ffn_b1")[:, g * FG * FC:(g + 1) * FG * FC][:, :, None].to_broadcast([P, FG * FC, BATCH]),
                   ALU.add).then_inc(pre_ready, 1)
                if g in (0, 3):
                    share_of(g // 3)
            dve.wait_ge(down_done, LOTS)
            tt(ffn_t[:, :, :], ms[:, HALF:HALF + EXPERTS * BATCH].rearrange("p (e b) -> p b e", b=BATCH),
               col("ffn_b2")[:, None, :].to_broadcast([P, BATCH, EXPERTS]), ALU.add).then_inc(ffnt_ready, 1)
            dve.wait_ge(ffn_turned, 1)
            nc.vector.tensor_copy(ffn_o[:, :, :].rearrange("p q c -> p (q c)"), ms[:, 0:2 * P]).then_inc(ffno_ready, 1)
            for q in range(2):
                dve.wait_ge(added_done, q + 1)
                tt(final[:, q * TOPK:(q + 1) * TOPK, :].rearrange("p k c -> p (k c)"),
                   picked[:, q * TOPK:(q + 1) * TOPK, :].rearrange("p k c -> p (k c)"), kps[q][:, :],
                   ALU.add).then_inc(final_ready, 1)

        @block.tensor
        def _(pe):
            mm, turn = nc.tensor.matmul, nc.tensor.transpose

            def turn_all(src, done):
                for g in range(GROUPS):
                    last = turn(ms[:, g * P:(g + 1) * P], src(g), ident[:, :])
                last.then_inc(done, 1)

            def key(i, ch):
                wait(pe, relu_done, i, CHUNKS, ch - 1)
                for h in range(2):
                    last = mm(kps[ch % 2][:, h * HALF:(h + 1) * HALF], w_key[:, ch * P:(ch + 1) * P],
                              y2[:, i[0] % 2, h * HALF:(h + 1) * HALF], start=True, stop=True)
                last.then_inc(key_done, 1)

            def value(i, ch):
                wait(pe, sq_done[SQUARES[ch]], i, SQ_N[SQUARES[ch]], SQ_K[ch])
                if ch == 0:
                    wait(pe, rk_ready, at(i, -1))
                for h in range(2):
                    last = mm(kv[:, h * HALF:(h + 1) * HALF], col("w_value")[:, ch * P:(ch + 1) * P],
                              hid[:, ch, h * HALF:(h + 1) * HALF], start=(ch == 0), stop=(ch == CHUNKS - 1))
                last.then_inc(value_done, 1)

            def step(i):
                f, b = at(i, 1), at(i, -1)
                m, fr, bk = real(i), real(f), real(b)
                if m:
                    wait(pe, y2_ready, i)
                    key(i, 0)
                if fr:
                    wait(pe, z_ready[1], f)
                    wait(pe, lg_ready, at(i, -2))
                    turn_all(lambda g: z1[:, g, :], z1_turned)
                if m:
                    key(i, 1)
                    if fr:
                        wait(pe, y1_ready, f)
                    else:
                        wait(pe, lg_ready, at(i, -2))
                    for h in range(2):
                        last = mm(ms[:, h * HALF:(h + 1) * HALF], w_recep[:, :],
                                  y2[:, i[0] % 2, h * HALF:(h + 1) * HALF], start=True, stop=True)
                    last.then_inc(recep_done, 1)
                    value(i, 0)
                if bk:
                    wait(pe, rk_ready, b)
                    if m:
                        wait(pe, recep_ready, i)
                    else:
                        wait(pe, lg_ready, at(i, -2))
                    turn_all(lambda g: rk[:, g * P:(g + 1) * P], rk_turned)
                if m:
                    key(i, 2)
                if fr:
                    wait(pe, silu_ready, f)
                    if bk:
                        wait(pe, x1_ready, b)
                    elif m:
                        wait(pe, recep_ready, i)
                    for g in range(GROUPS):
                        last = mm(ms[:, g * P:(g + 1) * P], sl[:, g * P:(g + 1) * P], w_out[:, :],
                                  start=True, stop=True)
                    last.then_inc(att_done, 1)
                if m:
                    value(i, 1)
                if bk:
                    wait(pe, z_ready[3], b)
                    if fr:
                        wait(pe, t1_ready, f)
                    turn_all(lambda g: z3[:, g, :], z3_turned)
                if m:
                    key(i, 3)
                    value(i, 2)
                if fr:
                    wait(pe, z_ready[2], f)
                    if bk:
                        wait(pe, tn_ready, b)
                    turn_all(lambda g: z2[:, g, :], z2_turned)
                if m:
                    value(i, 3)
                if bk:
                    wait(pe, tn_ready, b)
                    if fr:
                        wait(pe, y2_ready, f)
                    for h in range(2):
                        last = mm(ms[h * EXPERTS:(h + 1) * EXPERTS, 0:HALF], col("gate_w"),
                                  tn[:, h * HALF:(h + 1) * HALF], start=True, stop=True)
                    last.then_inc(gate_done, 1)

            pe.wait_ge(cst_loaded, 16)
            mm(kps[0][:, 0:HID], col("w_whiten"), col("w_key"), start=True, stop=True)
            mm(kps[1][:, 0:P], col("w_whiten"), col("w_recep"), start=True, stop=True).then_inc(fold_mm, 1)
            pe.wait_ge(fold_raw, 2)
            for ch in range(CHUNKS):
                mm(ms[:, ch:ch + 1], hid[:, 0, ch * P:(ch + 1) * P], col("b2"), start=True, stop=True)
            mm(ms[:, CHUNKS:CHUNKS + 1], hid[:, 1, 0:P], col("b2"), start=True, stop=True).then_inc(fold_bias, 1)
            pe.wait_ge(fold_ready, 5)
            pe.wait_ge(pool_const, 5)
            run_steps(pe, step)

            pe.wait_ge(rowb_ready, 1)
            for q in range(2):
                for k in range(TOPK):
                    last = turn(kps[q][:, k * P:(k + 1) * P], row_b[:, q * TOPK + k, :], ident[:, :])
                last.then_inc(row_turned, 1)
            pe.wait_ge(pooling, 1)
            for q in range(2):
                last = turn(ms[:, q * P:(q + 1) * P], pooled[:, q, 0, :], ident[:, :])
            last.then_inc(pool_turned, 1)
            pe.wait_ge(pooled_ready, 1)

            def up(g):
                pe.wait_ge(lot_loaded[g % RING], 16 * (g // RING + 1))
                if g >= 2:
                    pe.wait_ge(pre_ready, g - 1)
                for e in range(FG):
                    for f in range(FC):
                        o = 512 * (g % 2) + (e * FC + f) * BATCH
                        last = mm(kv[:, o:o + BATCH], ring[:, g % RING, e * FFN + f * P:e * FFN + (f + 1) * P],
                                  pooled_t[:, :, g * FG + e], start=True, stop=True)
                last.then_inc(up_done, 1)

            def down(g):
                pe.wait_ge(gelu_ready, g + 1)
                for e in range(FG):
                    o = HALF + (g * FG + e) * BATCH
                    for f in range(FC):
                        w = FG * FFN + (e * FC + f) * P
                        last = mm(ms[:, o:o + BATCH], ring[:, g % RING, w:w + P],
                                  hact[:, g % 2, (e * FC + f) * BATCH:(e * FC + f + 1) * BATCH],
                                  start=(f == 0), stop=(f == FC - 1))
                last.then_inc(down_done, 1)

            up(0)
            for g in range(1, LOTS):
                up(g)
                down(g - 1)
            down(LOTS - 1)
            pe.wait_ge(ffnt_ready, 1)
            for q in range(2):
                last = turn(ms[:, q * P:(q + 1) * P],
                            ffn_t[:, :, :].rearrange("p b e -> p (b e)")[:, q * P:(q + 1) * P], ident[:, :])
            last.then_inc(ffn_turned, 1)
            pe.wait_ge(ffno_ready, 1)
            for q in range(2):
                pe.wait_ge(sharing, q + 1)
                for k in range(TOPK):
                    last = mm(kps[q][:, k * P:(k + 1) * P], share[:, q, k * P:(k + 1) * P], ffn_o[:, q, :],
                              start=True, stop=True)
                last.then_inc(added_done, 1)


def kernel(**inputs):
    import numpy as np
    import concourse.bacc as bacc
    from concourse.bass_utils import run_bass_kernel_spmd

    a = {k: np.asarray(v) for k, v in inputs.items()}

    t = a["x"].reshape(2, 2, P, PAIR_UNITS, HALF // P, P).transpose(0, 3, 5, 1, 4, 2)
    x = np.ascontiguousarray(t).reshape(UNITS, P, GROUPS * P)

    c = np.empty((P, COLS), np.float32)
    parts = {
        "g0": np.broadcast_to(a["L0_conv_ln0_g"], (P, P)), "b0": np.broadcast_to(a["L0_conv_ln0_b"], (P, P)),
        "w_out": a["L0_conv_W_out"].T, "w_whiten": a["L0_conv_W_whiten"], "w_key": a["L0_conv_W_key"].T,
        "w_recep": a["L0_conv_W_recep"].T,
        "w_value": a["L0_conv_W_value"].T.reshape(CHUNKS, P, P).transpose(1, 0, 2).reshape(P, HID),
        "gate_w": a["L0_ffn_gate_w"].T, "g1": a["L0_conv_ln1_g"][:, None], "b1": a["L0_conv_ln1_b"][:, None],
        "g2": a["L0_conv_ln2_g"][:, None], "b2": a["L0_conv_ln2_b"][:, None],
        "gate_b": np.concatenate([a["L0_ffn_gate_b"]] * 2)[:, None],
        "ffn_b1": a["L0_ffn_weight1"][:, P, :].reshape(EXPERTS, FC, P).transpose(2, 0, 1).reshape(P, EXPERTS * FC),
        "ffn_b2": a["L0_ffn_weight2"][:, FFN, :].T,
    }
    for name, value in parts.items():
        c[:, COL[name][0]:COL[name][1]] = value

    w1 = a["L0_ffn_weight1"][:, :P, :].reshape(LOTS, FG, P, FFN).transpose(0, 2, 1, 3).reshape(LOTS, P, FG * FFN)
    w2 = a["L0_ffn_weight2"][:, :FFN, :].reshape(LOTS, FG, FC, P, P).transpose(0, 3, 1, 2, 4)
    wff = np.concatenate([w1, w2.reshape(LOTS, P, FG * FFN)], axis=2)

    nc = bacc.Bacc("TRN2", target_bir_lowering=False, num_devices=1)
    arrays = {"x_dram": x, "cst_dram": c, "wff_dram": np.ascontiguousarray(wff)}
    args = [nc.dram_tensor(n, v.shape, mybir.dt.from_np(v.dtype), kind="ExternalInput").ap() for n, v in arrays.items()]
    out = nc.dram_tensor("out_dram", x.shape, F32, kind="ExternalOutput").ap()
    metaformer_kernel(nc, *args, out)
    r = run_bass_kernel_spmd(nc, [arrays], core_ids=[0]).results[0]["out_dram"]
    y = np.asarray(r).reshape(2, PAIR_UNITS, P, 2, HALF // P, P).transpose(0, 3, 5, 1, 4, 2)
    return np.ascontiguousarray(y).reshape(BATCH, P, P, P)
```

```python
from contextlib import ExitStack

import concourse.bass as bass
from concourse import mybir

F32 = mybir.dt.float32
F32R = mybir.dt.float32r
U32 = mybir.dt.uint32
ALU = mybir.AluOpType
ACT = mybir.ActivationFunctionType
AX = mybir.AxisListType

P = 128
BATCH, TOKENS = 4, 128 * 128
HALF = 512
UNIT = 2 * HALF
GROUPS = UNIT // P
PAIR_UNITS = TOKENS // HALF
UNITS = BATCH // 2 * PAIR_UNITS
HID = 512
CHUNKS = HID // P
EXPERTS, TOPK, FFN = 64, 8, 512
FC = FFN // P
FG = 4
LOTS = EXPERTS // FG
LOT = FG * (FFN + FC * P)
RING = 5
RING_OWN = 3
CAND = PAIR_UNITS * TOPK

_at = 0
COL = {}
for _name, _n in (("g0", P), ("b0", P), ("w_out", P), ("w_whiten", P), ("w_key", HID), ("w_recep", P),
                  ("w_value", HID), ("gate_w", EXPERTS), ("g1", 1), ("b1", 1), ("g2", 1), ("b2", 1),
                  ("gate_b", 1), ("ffn_b1", EXPERTS * FC), ("ffn_b2", EXPERTS)):
    COL[_name] = (_at, _at + _n)
    _at += _n
COLS = _at

LN = {0: (1.0 + 1e-5, 1e-11), 1: (1.0, 1e-5), 2: (1.0, 1e-5), 3: (1.0, 1e-5)}
MEAN = {0: True, 1: True, 2: False, 3: False}
LN_STEPS = {0: 8, 1: 9, 2: 7, 3: 7}

UNROLL = 4
Z1_FIRST = 4
AHEAD, BEHIND = 4, 2
FIRST_LOOP, LAST_LOOP = 5, 56


def metaformer_kernel(nc, x, cst, wff, out):
    ctx = ExitStack()
    with ctx:
        def sb(name, shape, dt=F32):
            return ctx.enter_context(nc.sbuf_tensor(name, shape, dt))

        def sem(name):
            return ctx.enter_context(nc.semaphore(name))

        C = sb("constants", [P, COLS])
        ident = sb("ident", [P, P])
        w_out = sb("w_out_half", [P, P])
        w_kr = sb("w_key_recep", [P, HID + P])
        w_hi = sb("w_key_recep_hi", [P, HID + P], F32R)
        w_lo = sb("w_key_recep_lo", [P, HID + P], F32R)
        w_gate = sb("w_gate_centred", [P, EXPERTS])
        centre = sb("centre", [P, P])
        bias_kr = sb("bias_key_recep", [P, CHUNKS + 1])
        g_half = sb("minus_half", [P, 2 * TOPK])
        g_quarter = sb("quarter_scale", [P, 2, 2 * TOPK])

        def col(name):
            return C[:, COL[name][0]:COL[name][1]]

        xt = sb("x_tok", [P, 4, GROUPS, P])
        t0 = sb("t0_tok", [P, 2, GROUPS, P])
        z1 = sb("z1_tok", [P, GROUPS, P])
        t1 = sb("t1_tok", [P, GROUPS, P])
        res = sb("residual_tok", [P, 2, GROUPS, P])
        y2_hi = sb("y2_chan_hi", [P, 2, UNIT], F32R)
        y2_lo = sb("y2_chan_lo", [P, 2, UNIT], F32R)
        hid = sb("hidden", [P, CHUNKS, UNIT])
        x1 = sb("x1_tok", [P, 2, GROUPS, P])
        work = sb("work", [P, 2 * LOT])

        def tok(n):
            return work[:, n * UNIT:(n + 1) * UNIT].rearrange("p (g c) -> p g c", c=P)

        def chan(n):
            return work[:, n * UNIT:(n + 1) * UNIT]

        z0, z2, z3 = tok(0), tok(1), tok(2)
        y1, sl, gate_r, rk, tn = chan(3), chan(4), chan(5), chan(6), chan(7)
        lg = sb("logits", [P, HALF])
        ex = sb("exp_scratch", [P, HALF])
        st = [sb(f"stats{n}", [P, GROUPS, 6]) for n in range(4)]
        sm = [sb(f"sums{n}", [P, GROUPS, 2]) for n in range(4)]
        df = [sb(f"diffs{n}", [P, GROUPS]) for n in range(4)]
        va = [sb(f"var{n}", [P, GROUPS]) for n in range(4)]
        neg_mean = [sb(f"neg_mean{n}", [P, GROUPS]) for n in range(2)] + [None, None]
        shift1 = sb("shift1", [P, GROUPS])
        rstd = [sb(f"rstd{n}", [P, GROUPS]) for n in range(4)]

        mx = sb("unit_max8", [P, 2, TOPK])
        mi = sb("unit_index8", [P, 2, TOPK], U32)
        neg = sb("unit_neg_max", [P, 2])
        cval = sb("cand_values", [P, UNITS * TOPK])
        cidx = sb("cand_index", [P, UNITS * TOPK])
        csum = sb("unit_exp_sums", [P, UNITS])

        own = sb("expert_weights", [P, RING_OWN, LOT])
        ring = [own[:, n, :] for n in range(RING_OWN)] + [work[:, n * LOT:(n + 1) * LOT] for n in range(RING - RING_OWN)]

        iota_i = sb("iota_int", [P, 2, CAND], mybir.dt.int32)
        iota_f = sb("iota_pos_tile", [P, 2, CAND])
        half_bit = sb("half_bit", [P, 2 * TOPK], U32)
        v8 = sb("top_values", [P, 2, TOPK])
        pos = sb("top_pos", [P, 2, TOPK], U32)
        posf = sb("top_pos_f", [P, 2, TOPK])
        seq = sb("top_token", [P, 2 * TOPK])
        rows_t = sb("row_parts", [P, 4, 2 * TOPK], U32)
        rows = sb("rows", [P, 2 * TOPK], U32)
        rowsf = sb("rows_f", [P, 2 * TOPK])
        neg_m = sb("neg_top", [P, 2])
        e_max = sb("exp_unit_max", [P, 2, PAIR_UNITS])
        den = sb("denominator", [P, 2])
        rden = sb("rdenominator", [P, 2])
        prob = sb("probs", [P, 2, TOPK])
        g_st = sb("g_stats", [P, 2 * TOPK, 6])
        g_sm = sb("g_sums", [P, 2 * TOPK, 2])
        g_df = sb("g_diffs", [P, 2 * TOPK])
        g_va = sb("g_var", [P, 2 * TOPK])
        g_neg_mean = sb("g_mean", [P, 2 * TOPK])
        g_rstd = sb("g_rstd", [P, 2 * TOPK])
        pooled = sb("pooled", [P, 2, 2, P])
        pooled_t = sb("pooled_chan", [P, BATCH, EXPERTS])
        hpre = sb("expert_pre", [P, 2, FC * FG * BATCH])
        hact = sb("expert_hidden", [P, 2, FC * FG * BATCH])
        ffn_t = sb("expert_out_chan", [P, BATCH, EXPERTS])
        ffn_o = sb("expert_out", [P, 2, P])
        junk = ex[:, 0:CAND]
        junk2 = [t.rearrange("p a g c -> p (a g c)") for t in (xt[:, 2:4, :, :], t0[:, :, :, :])]
        picked = hid[:, 0:2, :].rearrange("p a (k c) -> p (a k) c", c=P)
        normed = hid[:, 2:4, :].rearrange("p a (k c) -> p (a k) c", c=P)
        row_b = xt[:, 0:2, :, :].rearrange("p a g c -> p (a g) c")
        row_all = t0[:, :, :, :].rearrange("p a g c -> p a (g c)")
        share = res[:, :, :, :].rearrange("p a g c -> p a (g c)")
        part = t1[:, :, :].rearrange("p g c -> p (g c)")
        up_sb = z1[:, :, :].rearrange("p (a g) c -> p a (g c)", a=2)
        down_sb = xt[:, 2:4, :, :].rearrange("p a g c -> p (a g) c")
        final = x1[:, :, :, :].rearrange("p a g c -> p (a g) c")

        kps = [ctx.enter_context(nc.psum_tensor(f"key{n}", [P, UNIT], F32)) for n in range(2)]
        kv = ctx.enter_context(nc.psum_tensor("kv", [P, UNIT], F32))
        ms = ctx.enter_context(nc.psum_tensor("misc", [P, UNIT], F32))

        cst_loaded = sem("cst_loaded")
        x_loaded = [sem(f"x_loaded{n}") for n in range(4)]
        x1_stored = [sem("x1_stored0"), sem("x1_stored1")]
        lot_loaded = [sem(f"lot_loaded{n}") for n in range(RING)]
        pool_const = sem("pool_const")
        fold_mm, fold_raw, fold_bias, fold_ready = sem("fold_mm"), sem("fold_raw"), sem("fold_bias"), sem("fold_ready")
        iota_ready = sem("iota_ready")
        stats_ready = [sem(f"stats_ready{n}") for n in range(4)]
        ln_steps = [sem(f"ln_steps{n}") for n in range(4)]
        z_ready = [sem(f"z_ready{n}") for n in range(4)]
        t0_steps = sem("t0_steps")
        z1_turned, y1_ready, tanh_ready, silu_ready = sem("z1_turned"), sem("y1_ready"), sem("tanh_ready"), sem("silu_ready")
        att_done, t1_ready, res_ready = sem("att_done"), sem("t1_ready"), sem("res_ready")
        z2_turned, y2_ready, y2_lo_ready = sem("z2_turned"), sem("y2_ready"), sem("y2_lo_ready")
        fold_centre, fold_mm2, fold_lo = sem("fold_centre"), sem("fold_mm2"), sem("fold_lo")
        up_copied, up_turned, down_copied = sem("up_copied"), sem("up_turned"), sem("down_copied")
        recep_done, recep_ready = sem("recep_done"), sem("recep_ready")
        key_done, relu_done, value_done = sem("key_done"), sem("relu_done"), sem("value_done")
        sq_done = sem("sq_done")
        rk_ready, rk_turned, x1_ready = sem("rk_ready"), sem("rk_turned"), sem("x1_ready")
        z3_turned, tn_ready = sem("z3_turned"), sem("tn_ready")
        gate_done, lg_ready = sem("gate_done"), sem("lg_ready")
        max_ready, index_ready, neg_ready, exp_ready, cand_kept = (
            sem("max_ready"), sem("index_ready"), sem("neg_ready"), sem("exp_ready"), sem("cand_kept"))
        pick, negm_ready, emax_ready, den_ready = sem("pick"), sem("negm_ready"), sem("emax_ready"), sem("den_ready")
        rows_ready, gathered, probs_ready = sem("rows_ready"), sem("gathered"), sem("probs_ready")
        g_stats_ready, g_ln, pooling, pool_turned = sem("g_stats_ready"), sem("g_ln"), sem("pooling"), sem("pool_turned")
        pooled_ready, up_done, pre_ready, gelu_ready, down_done = (
            sem("pooled_ready"), sem("up_done"), sem("pre_ready"), sem("gelu_ready"), sem("down_done"))
        rowb_ready, row_turned, row_copied = sem("rowb_ready"), sem("row_turned"), sem("row_copied")
        ffnt_ready, ffn_turned, ffno_ready, added_done, final_ready, scattered = (
            sem("ffnt_ready"), sem("ffn_turned"), sem("ffno_ready"), sem("added_done"), sem("final_ready"), sem("scattered"))

        def at(u, d):
            return (u[0] + d, u[1])

        def num(u):
            return u[0] if u[1] is None else u[1] * UNROLL + u[0]

        def real(u):
            return u[1] is not None or 0 <= u[0] < UNITS

        def wait(eng, s, u, per=1, k=None):
            v = per * u[0] + (per if k is None else k)
            if u[1] is not None:
                eng.wait_ge(s, u[1] * (UNROLL * per) + v)
            elif v > 0:
                eng.wait_ge(s, v)

        def wait_dma(eng, s, u, n):
            v = 16 * (u[0] // n + 1)
            if u[1] is not None:
                eng.wait_ge(s, u[1] * (16 * UNROLL // n) + v)
            elif v > 0:
                eng.wait_ge(s, v)

        def run_steps(eng, step):
            for i in range(-AHEAD, FIRST_LOOP):
                step((i, None))
            with eng.Fori(0, (LAST_LOOP - FIRST_LOOP + 1) // UNROLL) as j:
                for n in range(UNROLL):
                    step((FIRST_LOOP + n, j))
            for i in range(LAST_LOOP + 1, UNITS + BEHIND):
                step((i, None))

        block = ctx.enter_context(nc.Block())

        @block.sync
        def _(sp):
            def load_x(u):
                if real(u):
                    wait(sp, res_ready, at(u, -4))
                    sp.dma_start(xt[:, u[0] % 4, :, :].rearrange("p g c -> p (g c)"),
                                 x[bass.ds(num(u), 1), :, :].rearrange("a p n -> (a p) n")
                                 ).then_inc(x_loaded[u[0] % 4], 16)

            def step(i):
                b = at(i, -1)
                if real(b):
                    wait(sp, x1_ready, b, 2)
                    sp.dma_start(out[bass.ds(num(b), 1), :, :].rearrange("a p n -> (a p) n"),
                                 x1[:, b[0] % 2, :, :].rearrange("p g c -> p (g c)")
                                 ).then_inc(x1_stored[b[0] % 2], 16)
                load_x(at(i, 5))

            sp.dma_start(C[:, :], cst[:, :]).then_inc(cst_loaded, 16)
            load_x((0, None))
            for n in range(RING_OWN):
                sp.dma_start(ring[n], wff[n, :, :]).then_inc(lot_loaded[n], 16)
            run_steps(sp, step)
            sp.wait_ge(index_ready, UNITS)
            for g in range(RING_OWN, LOTS):
                if g >= RING:
                    sp.wait_ge(down_done, g - RING + 1)
                sp.dma_start(ring[g % RING], wff[g, :, :]).then_inc(lot_loaded[g % RING], 16)

        def ln_on_pool(pool, s, base, stat, sums, diff, var, neg_mu, shift, rs, exponent, quarter, scale, eps):
            tt, ts = nc.gpsimd.tensor_tensor, nc.gpsimd.tensor_scalar
            n = 5
            tt(out=sums, in0=stat[:, :, 1:3], in1=stat[:, :, 4:6], op=ALU.add).then_inc(s, 1)
            tt(out=diff, in0=stat[:, :, 1], in1=stat[:, :, 4], op=ALU.subtract).then_inc(s, 1)
            base(2)
            tt(out=diff, in0=diff, in1=diff, op=ALU.mult).then_inc(s, 1)
            ts(var, sums[:, :, 1], scale / P, eps, ALU.mult, ALU.add).then_inc(s, 1)
            if neg_mu is not None:
                ts(neg_mu, sums[:, :, 0], -0.5, None, ALU.mult).then_inc(s, 1)
                n = 6
            base(3)
            tt(out=diff, in0=diff, in1=quarter, op=ALU.mult).then_inc(s, 1)
            base(n)
            tt(out=var, in0=var, in1=diff, op=ALU.add).then_inc(s, 1)
            base(n + 1)
            tt(out=rs, in0=var, in1=exponent, op=ALU.pow).then_inc(s, 1)
            if shift is not None:
                base(n + 2)
                tt(out=shift, in0=neg_mu, in1=rs, op=ALU.mult).then_inc(s, 1)

        @block.gpsimd
        def _(pool):
            def ln(n, u):
                wait(pool, stats_ready[n], u)
                wait(pool, z_ready[n], at(u, -1))
                ln_on_pool(pool, ln_steps[n], lambda k: wait(pool, ln_steps[n], u, LN_STEPS[n], k),
                           st[n][:, :, :], sm[n][:, :, :], df[n][:, :], va[n][:, :],
                           neg_mean[n][:, :] if MEAN[n] else None, shift1[:, :] if n == 1 else None, rstd[n][:, :],
                           g_half[:, 0:GROUPS], g_quarter[:, min(n, 1), 0:GROUPS], *LN[n])

            def step(i):
                d, a, f, b, c = at(i, 4), at(i, 3), at(i, 2), at(i, -1), at(i, -2)
                if real(a):
                    wait(pool, z_ready[0], a)
                    wait(pool, t1_ready, at(a, -2), 2)
                    nc.gpsimd.tensor_tensor(out=z0, in0=z0, in1=col("g0")[:, None, :].to_broadcast([P, GROUPS, P]),
                                            op=ALU.mult).then_inc(t0_steps, 1)
                    wait(pool, t0_steps, a, 2, 1)
                    nc.gpsimd.tensor_tensor(out=t0[:, a[0] % 2, :, :], in0=z0,
                                            in1=col("b0")[:, None, :].to_broadcast([P, GROUPS, P]),
                                            op=ALU.add).then_inc(t0_steps, 1)
                if real(b):
                    ln(3, b)
                if real(a):
                    ln(1, a)
                if real(d):
                    ln(0, d)
                if real(f):
                    ln(2, f)
                if real(c):
                    wait(pool, index_ready, c)
                    v = num(c) * TOPK
                    nc.gpsimd.tensor_copy(cval[:, bass.ds(v, TOPK)], mx[:, c[0] % 2, :]).then_inc(cand_kept, 1)
                    nc.gpsimd.tensor_copy(cidx[:, bass.ds(v, TOPK)], mi[:, c[0] % 2, :]).then_inc(cand_kept, 1)

            nc.gpsimd.memset(ident[:, :], 0.0).then_inc(pool_const, 1)
            nc.gpsimd.memset(g_half[:, :], -0.5).then_inc(pool_const, 1)
            for n in range(2):
                nc.gpsimd.memset(g_quarter[:, n, :], LN[n][0] / 4).then_inc(pool_const, 1)
            pool.wait_ge(pool_const, 4)
            nc.gpsimd.affine_select(out=ident[:, :], in_=ident[:, :], compare_op=ALU.not_equal, fill=1.0, base=0,
                                    pattern=[[-1, P]], channel_multiplier=1).then_inc(pool_const, 1)
            nc.gpsimd.iota(iota_i[:, 0, :], pattern=[[1, CAND]], base=0, channel_multiplier=0).then_inc(pool_const, 1)
            nc.gpsimd.iota(iota_i[:, 1, :], pattern=[[HALF, PAIR_UNITS], [0, TOPK]], base=0,
                           channel_multiplier=0).then_inc(pool_const, 1)
            nc.gpsimd.iota(half_bit[:, :], pattern=[[0, 2 * TOPK]], base=0, channel_multiplier=1).then_inc(pool_const, 1)
            pool.wait_ge(pool_const, 8)
            nc.gpsimd.tensor_copy(iota_f[:, :, :], iota_i[:, :, :]).then_inc(iota_ready, 1)
            pool.wait_ge(cst_loaded, 16)
            run_steps(pool, step)

            for par in range(2):
                pool.wait_ge(x1_stored[par], 16 * (UNITS // 2))
            for q in range(2):
                pool.wait_ge(rows_ready, q + 1)
                for k in range(TOPK):
                    nc.gpsimd.indirect_dma_start(
                        out=picked[:, q * TOPK + k, :], out_offset=None, in_=out.rearrange("u p (g c) -> (u p g) c", c=P),
                        in_offset=bass.IndirectOffsetOnAxis(ap=rows[:, q * TOPK + k:q * TOPK + k + 1], axis=0)
                    ).then_inc(gathered, 16)
            pool.wait_ge(g_stats_ready, 1)
            ln_on_pool(pool, g_ln, lambda k: pool.wait_ge(g_ln, k), g_st[:, :, :], g_sm[:, :, :], g_df[:, :],
                       g_va[:, :], g_neg_mean[:, :], None, g_rstd[:, :], g_half[:, :], g_quarter[:, 1, :], *LN[3])
            for q in range(2):
                pool.wait_ge(final_ready, q + 1)
                for k in range(TOPK):
                    if q or k:
                        pool.wait_ge(scattered, 16 * (q * TOPK + k))
                    nc.gpsimd.indirect_dma_start(
                        out=out.rearrange("u p (g c) -> (u p g) c", c=P),
                        out_offset=bass.IndirectOffsetOnAxis(ap=rows[:, q * TOPK + k:q * TOPK + k + 1], axis=0),
                        in_=final[:, q * TOPK + k, :], in_offset=None).then_inc(scattered, 16)
            pool.wait_ge(scattered, 16 * 2 * TOPK)

        @block.scalar
        def _(act):
            def relu(i, ch):
                wait(act, key_done, i, CHUNKS, ch + 1)
                wait(act, value_done, at(i, -1), CHUNKS, ch + 1)
                nc.scalar.activation(hid[:, ch, :], kps[ch % 2][:, :], ACT.Relu,
                                     bias=bias_kr[:, ch:ch + 1]).then_inc(relu_done, 1)

            def square(i, ch):
                wait(act, relu_done, i, CHUNKS, ch + 1)
                nc.scalar.activation(hid[:, ch, :], hid[:, ch, :], ACT.Square).then_inc(sq_done, 1)

            def scale_z1(u, groups):
                for g in groups:
                    last = nc.scalar.activation(z1[:, g, :], t0[:, u[0] % 2, g, :], ACT.Identity,
                                                bias=shift1[:, g:g + 1], scale=rstd[1][:, g:g + 1])
                if g == GROUPS - 1:
                    last.then_inc(z_ready[1], 1)

            def step(i):
                a, f, e, c = at(i, 3), at(i, 2), at(i, 1), at(i, -2)
                if real(i):
                    relu(i, 1)
                if real(c):
                    wait(act, z3_turned, c)
                    wait(act, gate_done, at(c, -1))
                    nc.scalar.activation(tn, ms[:, :], ACT.Copy).then_inc(tn_ready, 1)
                if real(i):
                    square(i, 1)
                if real(f):
                    scale_z1(f, range(Z1_FIRST, GROUPS))
                if real(i):
                    relu(i, 2)
                    square(i, 2)
                if real(e):
                    wait(act, z2_turned, e)
                    wait(act, recep_done, at(e, -2))
                    wait(act, key_done, at(e, -2), CHUNKS)
                    nc.scalar.activation(y2_hi[:, e[0] % 2, :], ms[:, :], ACT.Copy).then_inc(y2_ready, 1)
                if real(i):
                    relu(i, 3)
                if real(i):
                    square(i, 3)
                if real(f):
                    wait(act, z1_turned, f)
                    wait(act, silu_ready, at(f, -1))
                    nc.scalar.activation(y1, ms[:, :], ACT.Identity, bias=col("b1"),
                                         scale=col("g1")).then_inc(y1_ready, 1)
                if real(f):
                    wait(act, y1_ready, f)
                    wait(act, att_done, at(f, -1))
                    nc.scalar.activation(sl, y1, ACT.Tanh, scale=0.5).then_inc(tanh_ready, 1)
                if real(c):
                    wait(act, gate_done, c)
                    wait(act, index_ready, at(c, -1))
                    wait(act, exp_ready, at(c, -1))
                    nc.scalar.activation(lg[:, :], ms[:, 0:HALF], ACT.Identity,
                                         bias=col("gate_b")).then_inc(lg_ready, 1)
                if real(i):
                    wait(act, recep_done, i)
                    wait(act, rk_ready, at(i, -1))
                    nc.scalar.activation(gate_r, ms[:, :], ACT.Tanh, bias=bias_kr[:, CHUNKS:CHUNKS + 1],
                                         scale=0.5).then_inc(recep_ready, 1)
                if real(e):
                    relu(e, 0)
                    square(e, 0)
                if real(c):
                    wait(act, neg_ready, c)
                    nc.scalar.activation(ex[:, :], lg[:, :], ACT.Exp, bias=neg[:, c[0] % 2:c[0] % 2 + 1],
                                         accum_out=csum[:, bass.ds(num(c), 1)]).then_inc(exp_ready, 1)
                if real(a):
                    wait(act, z1_turned, at(a, -1))
                    wait(act, ln_steps[1], a, LN_STEPS[1])
                    scale_z1(a, range(Z1_FIRST))

            act.wait_ge(cst_loaded, 16)
            act.wait_ge(fold_mm, 1)
            nc.scalar.activation(hid[:, 0, 0:HID], kps[0][:, 0:HID], ACT.Copy).then_inc(fold_raw, 1)
            nc.scalar.activation(hid[:, 0, HID:HID + P], kps[0][:, HID:HID + P], ACT.Copy).then_inc(fold_raw, 1)
            nc.scalar.activation(hid[:, 1, 0:HID + P], kps[0][:, 0:HID + P], ACT.Identity,
                                 scale=col("g2")).then_inc(fold_raw, 1)
            nc.scalar.activation(w_out[:, :], col("w_out"), ACT.Copy, scale=0.5).then_inc(fold_ready, 1)
            act.wait_ge(fold_bias, 1)
            nc.scalar.activation(bias_kr[:, 0:CHUNKS], ms[:, 0:CHUNKS], ACT.Copy).then_inc(fold_ready, 1)
            nc.scalar.activation(bias_kr[:, CHUNKS:CHUNKS + 1], ms[:, CHUNKS:CHUNKS + 1], ACT.Copy,
                                 scale=0.5).then_inc(fold_ready, 1)
            act.wait_ge(fold_mm2, 1)
            nc.scalar.activation(w_kr[:, :], kps[1][:, 0:HID + P], ACT.Copy).then_inc(fold_ready, 1)
            nc.scalar.activation(w_hi[:, :], kps[1][:, 0:HID + P], ACT.Copy).then_inc(fold_ready, 1)
            nc.scalar.activation(w_gate[:, :], kv[:, 0:EXPERTS], ACT.Copy).then_inc(fold_ready, 1)
            act.wait_ge(fold_ready, 6)
            run_steps(act, step)

            act.wait_ge(cand_kept, 2 * UNITS)
            act.wait_ge(negm_ready, 1)
            for q in range(2):
                nc.scalar.activation(
                    e_max[:, q, :], cval[:, q * CAND:(q + 1) * CAND].rearrange("p (u k) -> p u k", k=TOPK)[:, :, 0],
                    ACT.Exp, bias=neg_m[:, q:q + 1]).then_inc(emax_ready, 1)
                nc.scalar.activation(prob[:, q, :], v8[:, q, :], ACT.Exp, bias=neg_m[:, q:q + 1]).then_inc(emax_ready, 1)
            for q in range(2):
                act.wait_ge(row_turned, q + 1)
                nc.scalar.activation(row_all[:, q, :], kps[q][:, :], ACT.Copy).then_inc(row_copied, 1)

            def copy_up(g):
                act.wait_ge(up_done, g + 1)
                if g >= 2:
                    act.wait_ge(up_turned, g - 1)
                nc.scalar.activation(up_sb[:, g % 2, :], kv[:, HALF * (g % 2):HALF * (g % 2 + 1)],
                                     ACT.Copy).then_inc(up_copied, 1)

            copy_up(0)
            for g in range(LOTS):
                if g + 1 < LOTS:
                    copy_up(g + 1)
                act.wait_ge(pre_ready, g + 1)
                if g >= 2:
                    act.wait_ge(down_done, g - 1)
                nc.scalar.activation(hact[:, g % 2, :], hpre[:, g % 2, :], ACT.Gelu).then_inc(gelu_ready, 1)

        @block.vector
        def _(dve):
            ts, tt, stt = nc.vector.tensor_scalar, nc.vector.tensor_tensor, nc.vector.scalar_tensor_tensor

            def half(t, h):
                return t[:, h * (GROUPS // 2):(h + 1) * (GROUPS // 2), :]

            def stats(n, src, source_ready=None):
                for g in range(GROUPS):
                    if source_ready and g % (GROUPS // 2) == 0:
                        source_ready(g // (GROUPS // 2))
                    last = nc.vector.bn_stats(st[n][:, g, :], src[:, g, :])
                last.then_inc(stats_ready[n], 1)

            def scale_rows(n, dst, src, u):
                wait(dve, ln_steps[n], u, LN_STEPS[n])
                tt(dst, src, rstd[n][:, :, None].to_broadcast([P, GROUPS, P]),
                   ALU.mult).then_inc(z_ready[n], 1)

            def flat(t):
                return t.rearrange("p g c -> p (g c)")

            def step(i):
                d, a, f, e, b, c = at(i, 4), at(i, 3), at(i, 2), at(i, 1), at(i, -1), at(i, -2)
                if real(e):
                    wait(dve, z2_turned, at(e, -1))
                    scale_rows(2, z2, t1[:, :, :], e)
                if real(b):
                    wait(dve, rk_turned, b)
                    wait_dma(dve, x1_stored[b[0] % 2], at(b, -2), 2)
                    for h in range(2):
                        tt(flat(half(x1[:, b[0] % 2, :, :], h)), flat(half(res[:, b[0] % 2, :, :], h)),
                           ms[:, h * HALF:(h + 1) * HALF], ALU.add).then_inc(x1_ready, 1)
                if real(b):
                    stats(3, x1[:, b[0] % 2, :, :], lambda h: wait(dve, x1_ready, b, 2, h + 1))
                if real(e):
                    wait(dve, y2_ready, e)
                    wait(dve, recep_done, at(e, -2))
                    for h in range(2):
                        w = slice(h * HALF, (h + 1) * HALF)
                        tt(y2_lo[:, e[0] % 2, w], ms[:, w], y2_hi[:, e[0] % 2, w].bitcast(F32),
                           ALU.subtract).then_inc(y2_lo_ready, 1)
                    stt(out=flat(res[:, e[0] % 2, :, :]), in0=flat(t1[:, :, :]), scalar=2.0,
                        in1=flat(xt[:, e[0] % 4, :, :]), op0=ALU.mult, op1=ALU.add).then_inc(res_ready, 1)
                if real(a):
                    wait(dve, t0_steps, a, 2)
                    stats(1, t0[:, a[0] % 2, :, :])
                if real(b):
                    wait(dve, z3_turned, at(b, -1))
                    scale_rows(3, z3, x1[:, b[0] % 2, :, :], b)
                if real(d):
                    wait_dma(dve, x_loaded[d[0] % 4], d, 4)
                    stats(0, xt[:, d[0] % 4, :, :])
                if real(c):
                    wait(dve, cand_kept, at(c, -2), 2)
                    wait(dve, exp_ready, at(c, -2))
                    wait(dve, lg_ready, c)
                if real(f):
                    wait(dve, tanh_ready, f)
                    stt(out=sl, in0=sl, scalar=1.0, in1=y1, op0=ALU.add, op1=ALU.mult).then_inc(silu_ready, 1)
                if real(c):
                    nc.vector.max(mx[:, c[0] % 2, :], lg[:, :]).then_inc(max_ready, 1)
                    wait(dve, max_ready, c)
                    ts(neg[:, c[0] % 2:c[0] % 2 + 1], mx[:, c[0] % 2, 0:1], -1.0, None, ALU.mult).then_inc(neg_ready, 1)
                if real(i):
                    wait(dve, value_done, i, CHUNKS)
                    wait(dve, recep_ready, i)
                    wait(dve, rk_turned, at(i, -1))
                    stt(out=rk, in0=gate_r, scalar=1.0, in1=kv[:, :], op0=ALU.add,
                        op1=ALU.mult).then_inc(rk_ready, 1)
                if real(f):
                    wait(dve, att_done, f)
                    wait(dve, res_ready, at(f, -1))
                    for h in range(2):
                        tt(flat(half(t1[:, :, :], h)), flat(half(t0[:, f[0] % 2, :, :], h)),
                           ms[:, h * HALF:(h + 1) * HALF], ALU.add).then_inc(t1_ready, 1)
                    stats(2, t1, lambda h: wait(dve, t1_ready, f, 2, h + 1))
                if real(d):
                    wait(dve, ln_steps[0], d, LN_STEPS[0])
                    wait(dve, t0_steps, a, 2)
                    for g in range(GROUPS):
                        last = ts(z0[:, g, :], xt[:, d[0] % 4, g, :], neg_mean[0][:, g:g + 1],
                                  rstd[0][:, g:g + 1], ALU.add, ALU.mult)
                    last.then_inc(z_ready[0], 1)
                if real(c):
                    nc.vector.max_index(mi[:, c[0] % 2, :], mx[:, c[0] % 2, :], lg[:, :]).then_inc(index_ready, 1)

            dve.wait_ge(pool_const, 5)
            ts(centre[:, :], ident[:, :], -1.0 / P, None, ALU.add).then_inc(fold_centre, 1)
            dve.wait_ge(fold_ready, 5)
            tt(w_lo[:, :], w_kr[:, :], w_hi[:, :].bitcast(F32), ALU.subtract).then_inc(fold_lo, 1)
            run_steps(dve, step)

            count = [0]

            def then(ins):
                count[0] += 1
                ins.then_inc(pick, 1)
                dve.wait_ge(pick, count[0])

            dve.wait_ge(cand_kept, 2 * UNITS)
            dve.wait_ge(exp_ready, UNITS)
            dve.wait_ge(iota_ready, 1)
            then(ts(half_bit[:, :], half_bit[:, :], 6, 2, ALU.logical_shift_right, ALU.logical_shift_left))
            vals = [cval[:, q * CAND:(q + 1) * CAND] for q in range(2)]
            idxs = cidx[:, :].rearrange("p (q n) -> p q n", q=2)
            nc.vector.max(v8[:, 0, :], vals[0])
            then(nc.vector.max(v8[:, 1, :], vals[1]))
            ts(neg_m[:, :], v8[:, :, 0], -1.0, None, ALU.mult).then_inc(negm_ready, 1)
            nc.vector.max_index(pos[:, 0, :], v8[:, 0, :], vals[0])
            tt(idxs, idxs, iota_f[:, 1:2, :].to_broadcast([P, 2, CAND]), ALU.add)
            then(nc.vector.max_index(pos[:, 1, :], v8[:, 1, :], vals[1]))
            then(nc.vector.tensor_copy(posf[:, :, :], pos[:, :, :]))
            for q in range(2):
                for k in range(TOPK):
                    last = stt(out=junk2[q][:, k * CAND:(k + 1) * CAND], in0=iota_f[:, 0, :], scalar=posf[:, q, k:k + 1], in1=idxs[:, q, :],
                               op0=ALU.is_equal, op1=ALU.mult, accum_out=seq[:, q * TOPK + k:q * TOPK + k + 1])
            then(last)
            r = rows_t[:, :, :]
            then(nc.vector.tensor_copy(r[:, 0, :], seq[:, :]))
            ts(r[:, 1, :], r[:, 0, :], 9, 10, ALU.logical_shift_right, ALU.logical_shift_left)
            ts(r[:, 2, :], r[:, 0, :], P - 1, 3, ALU.bitwise_and, ALU.logical_shift_left)
            then(ts(r[:, 3, :], r[:, 0, :], 7, 3, ALU.logical_shift_right, ALU.bitwise_and))
            tt(r[:, 1, :], r[:, 1, :], r[:, 2, :], ALU.bitwise_or)
            then(tt(r[:, 3, :], r[:, 3, :], half_bit[:, :], ALU.bitwise_or))
            then(tt(r[:, 1, :], r[:, 1, :], r[:, 3, :], ALU.bitwise_or))
            for q in range(2):
                w = slice(q * TOPK, (q + 1) * TOPK)
                ts(rows[:, w], r[:, 1, w], q * 2 * TOKENS, None, ALU.bitwise_or).then_inc(rows_ready, 1)
            dve.wait_ge(rows_ready, 2)
            then(nc.vector.tensor_copy(rowsf[:, :], rows[:, :]))
            for q in range(2):
                dve.wait_ge(emax_ready, 2 * q + 2)
                then(stt(out=junk[:, q * PAIR_UNITS:(q + 1) * PAIR_UNITS], in0=e_max[:, q, :], scalar=1.0,
                         in1=csum[:, q * PAIR_UNITS:(q + 1) * PAIR_UNITS], op0=ALU.mult, op1=ALU.mult,
                         accum_out=den[:, q:q + 1]))
                then(nc.vector.reciprocal(rden[:, q:q + 1], den[:, q:q + 1]))
                then(ts(prob[:, q, :], prob[:, q, :], rden[:, q:q + 1], None, ALU.mult))
            for n in range(2 * TOPK):
                last = nc.vector.tensor_copy(row_b[:, n, :], rowsf[:, n:n + 1].to_broadcast([P, P]))
            last.then_inc(rowb_ready, 1)
            dve.wait_ge(gathered, 16 * 2 * TOPK)
            for n in range(2 * TOPK):
                last = nc.vector.bn_stats(g_st[:, n, :], picked[:, n, :])
            last.then_inc(g_stats_ready, 1)
            dve.wait_ge(g_ln, LN_STEPS[0])
            for n in range(2 * TOPK):
                last = ts(normed[:, n, :], picked[:, n, :], g_neg_mean[:, n:n + 1], g_rstd[:, n:n + 1],
                          ALU.add, ALU.mult)
            then(last)
            for k in range(TOPK):
                for q in range(2):
                    if k == 0:
                        last = ts(pooled[:, q, 0, :], normed[:, q * TOPK, :], prob[:, q, 0:1], None, ALU.mult)
                    else:
                        last = stt(out=pooled[:, q, k % 2, :], in0=normed[:, q * TOPK + k, :],
                                   scalar=prob[:, q, k:k + 1], in1=pooled[:, q, (k - 1) % 2, :],
                                   op0=ALU.mult, op1=ALU.add)
                then(last)
            nc.vector.tensor_copy(pooled[:, :, 0, :], pooled[:, :, 1, :]).then_inc(pooling, 1)
            dve.wait_ge(pool_turned, 1)
            nc.vector.tensor_copy(pooled_t[:, :, :].rearrange("p b e -> p (b e)"), ms[:, 0:2 * P]).then_inc(pooled_ready, 1)

            def add_share(q, k):
                if k == 0:
                    dve.wait_ge(row_copied, q + 1)
                dst = part if k else share[:, q, :]
                then(ts(dst, row_all[:, q, :], rowsf[:, q * TOPK + k:q * TOPK + k + 1], prob[:, q, k:k + 1],
                        ALU.is_equal, ALU.mult))
                if k:
                    then(tt(share[:, q, :], share[:, q, :], part, ALU.add))

            b1 = col("ffn_b1").rearrange("p (g e f) -> p g f e", g=LOTS, e=FG)
            for g in range(LOTS):
                add_share(g // TOPK, g % TOPK)
                dve.wait_ge(up_turned, g + 1)
                if g >= 2:
                    dve.wait_ge(gelu_ready, g - 1)
                tt(hpre[:, g % 2, :].rearrange("p (f e b) -> p f e b", f=FC, e=FG),
                   kps[0][:, HALF * (g % 2):HALF * (g % 2 + 1)].rearrange("p (f e r) -> p f e r", f=FC, e=FG)[:, :, :, 0:BATCH],
                   b1[:, g, :, :][:, :, :, None].to_broadcast([P, FC, FG, BATCH]), ALU.add).then_inc(pre_ready, 1)
            half = LOTS // 2
            for n, src in enumerate((kps[1], ms)):
                dve.wait_ge(down_done, half * (n + 1))
                nc.vector.tensor_copy(down_sb[:, n * half:(n + 1) * half, :].rearrange("p g c -> p (g c)"),
                                      src[:, :]).then_inc(down_copied, 1)
            dve.wait_ge(ffn_turned, 1)
            for n, src in enumerate((kv, kps[0])):
                for b in range(BATCH):
                    last = tt(ffn_t[:, b, n * half * FG:(n + 1) * half * FG].rearrange("p (g e) -> p g e", e=FG),
                              src[:, :].rearrange("p (g e r) -> p g e r", e=FG, r=32)[:, :, :, b],
                              col("ffn_b2")[:, n * half * FG:(n + 1) * half * FG].rearrange("p (g e) -> p g e", e=FG),
                              ALU.add)
            last.then_inc(ffnt_ready, 1)
            dve.wait_ge(ffn_turned, 2)
            nc.vector.tensor_copy(ffn_o[:, :, :].rearrange("p q c -> p (q c)"), ms[:, 0:2 * P]).then_inc(ffno_ready, 1)
            for q in range(2):
                dve.wait_ge(added_done, q + 1)
                tt(final[:, q * TOPK:(q + 1) * TOPK, :].rearrange("p k c -> p (k c)"),
                   picked[:, q * TOPK:(q + 1) * TOPK, :].rearrange("p k c -> p (k c)"), kps[q][:, :],
                   ALU.add).then_inc(final_ready, 1)

        @block.tensor
        def _(pe):
            mm, turn = nc.tensor.matmul, nc.tensor.transpose

            def wait_first(h, *turns):
                for s, u in turns:
                    if real(u):
                        if s in (t1_ready, x1_ready, y2_lo_ready):
                            wait(pe, s, u, 2, h + 1)
                        elif h == 0:
                            wait(pe, s, u)
                        return

            def turn_all(src, done, *turns):
                for g in range(GROUPS):
                    if g % (GROUPS // 2) == 0:
                        wait_first(g // (GROUPS // 2), *turns)
                    last = turn(ms[:, g * P:(g + 1) * P], src(g), ident[:, :])
                last.then_inc(done, 1)

            def project(dst, i, w, first, halves=(0, 1)):
                for h in halves:
                    for n, (wt, y) in enumerate(((w_hi, y2_hi), (w_lo, y2_hi), (w_hi, y2_lo))):
                        if first and n == 2:
                            wait(pe, y2_lo_ready, i, 2, h + 1)
                        last = mm(dst[:, h * HALF:(h + 1) * HALF], wt[:, w:w + P],
                                  y[:, i[0] % 2, h * HALF:(h + 1) * HALF], start=(n == 0), stop=(n == 2))
                return last

            def key(i, ch):
                wait(pe, relu_done, i, CHUNKS, ch - 1)
                project(kps[ch % 2], i, ch * P, ch == 0).then_inc(key_done, 1)

            def value(i, ch, halves=(0, 1)):
                wait(pe, sq_done, i, CHUNKS, ch + 1)
                if ch == 0:
                    wait(pe, rk_ready, at(i, -1))
                for h in halves:
                    last = mm(kv[:, h * HALF:(h + 1) * HALF], col("w_value")[:, ch * P:(ch + 1) * P],
                              hid[:, ch, h * HALF:(h + 1) * HALF], start=(ch == 0), stop=(ch == CHUNKS - 1))
                if halves[-1] == 1:
                    last.then_inc(value_done, 1)

            def step(i):
                f, e, b, c = at(i, 2), at(i, 1), at(i, -1), at(i, -2)
                if real(i):
                    key(i, 1)
                if real(c):
                    wait(pe, z_ready[3], c)
                    turn_all(lambda g: z3[:, g, :], z3_turned,
                             (t1_ready, at(f, -1)), (recep_ready, at(i, -1)), (lg_ready, at(c, -1)))
                if real(i):
                    value(i, 0)
                    key(i, 2)
                if real(b):
                    wait(pe, rk_ready, b)
                    turn_all(lambda g: rk[:, g * P:(g + 1) * P], rk_turned, (tn_ready, c), (t1_ready, at(f, -1)))
                if real(i):
                    value(i, 1)
                if real(e):
                    wait(pe, z_ready[2], e)
                    turn_all(lambda g: z2[:, g, :], z2_turned, (x1_ready, b), (t1_ready, at(f, -1)))
                if real(i):
                    key(i, 3)
                    value(i, 2, (0,))
                if real(f):
                    wait(pe, z_ready[1], f)
                    turn_all(lambda g: z1[:, g, :], z1_turned, (y2_lo_ready, e))
                if real(i):
                    value(i, 2, (1,))
                    value(i, 3, (0,))
                if real(c):
                    wait(pe, tn_ready, c)
                    wait_first(0, (y1_ready, f), (y2_lo_ready, e), (x1_ready, b))
                    for h in range(2):
                        last = mm(ms[h * EXPERTS:(h + 1) * EXPERTS, 0:HALF], w_gate[:, :],
                                  tn[:, h * HALF:(h + 1) * HALF], start=True, stop=True)
                    last.then_inc(gate_done, 1)
                if real(i):
                    value(i, 3, (1,))
                    wait_first(1, (y1_ready, f), (y2_lo_ready, e), (x1_ready, b))
                    if not real(c):
                        wait(pe, y1_ready, f)
                    project(ms, i, HID, False, (1,))
                    wait_first(0, (lg_ready, c))
                    project(ms, i, HID, False, (0,)).then_inc(recep_done, 1)
                if real(e):
                    wait(pe, y2_ready, e)
                    key(e, 0)
                if real(f):
                    wait(pe, silu_ready, f)
                    wait_first(0, (recep_ready, i), (y1_ready, f))
                    for g in range(GROUPS):
                        last = mm(ms[:, g * P:(g + 1) * P], sl[:, g * P:(g + 1) * P], w_out[:, :],
                                  start=True, stop=True)
                    last.then_inc(att_done, 1)

            pe.wait_ge(cst_loaded, 16)
            mm(kps[0][:, 0:HID], col("w_whiten"), col("w_key"), start=True, stop=True)
            mm(kps[0][:, HID:HID + P], col("w_whiten"), col("w_recep"), start=True, stop=True).then_inc(fold_mm, 1)
            pe.wait_ge(fold_raw, 3)
            for ch in range(CHUNKS + 1):
                last = mm(ms[:, ch:ch + 1], hid[:, 0, ch * P:(ch + 1) * P], col("b2"), start=True, stop=True)
            last.then_inc(fold_bias, 1)
            pe.wait_ge(fold_centre, 1)
            mm(kps[1][:, 0:HID], centre[:, :], hid[:, 1, 0:HID], start=True, stop=True)
            mm(kps[1][:, HID:HID + P], centre[:, :], hid[:, 1, HID:HID + P], start=True, stop=True)
            mm(kv[:, 0:EXPERTS], centre[:, :], col("gate_w"), start=True, stop=True).then_inc(fold_mm2, 1)
            pe.wait_ge(fold_ready, 6)
            pe.wait_ge(fold_lo, 1)
            run_steps(pe, step)

            pe.wait_ge(rowb_ready, 1)
            for q in range(2):
                for k in range(TOPK):
                    last = turn(kps[q][:, k * P:(k + 1) * P], row_b[:, q * TOPK + k, :], ident[:, :])
                last.then_inc(row_turned, 1)
            pe.wait_ge(pooling, 1)
            for q in range(2):
                last = turn(ms[:, q * P:(q + 1) * P], pooled[:, q, 0, :], ident[:, :])
            last.then_inc(pool_turned, 1)
            pe.wait_ge(pooled_ready, 1)

            def up(g):
                pe.wait_ge(lot_loaded[g % RING], 16 * (g // RING + 1))
                if g >= 2:
                    pe.wait_ge(up_copied, g - 1)
                for e in range(FG):
                    last = mm(kv[32 * e:32 * e + BATCH, HALF * (g % 2):HALF * (g % 2 + 1)],
                              pooled_t[:, :, g * FG + e], ring[g % RING][:, e * FFN:(e + 1) * FFN],
                              start=True, stop=True)
                last.then_inc(up_done, 1)

            def turn_up(g):
                pe.wait_ge(up_copied, g + 1)
                if g >= 2:
                    pe.wait_ge(pre_ready, g - 1)
                else:
                    pe.wait_ge(row_copied, 2)
                for f in range(FC):
                    o = HALF * (g % 2) + f * P
                    last = turn(kps[0][:, o:o + P], up_sb[:, g % 2, f * P:(f + 1) * P], ident[:, :])
                last.then_inc(up_turned, 1)

            def down(g):
                pe.wait_ge(gelu_ready, g + 1)
                dst, o = (kps[1], ms)[g // (LOTS // 2)], g % (LOTS // 2) * P
                for e in range(FG):
                    for f in range(FC):
                        w = FG * FFN + (e * FC + f) * P
                        last = mm(dst[32 * e:32 * e + BATCH, o:o + P],
                                  hact[:, g % 2, (f * FG + e) * BATCH:(f * FG + e + 1) * BATCH],
                                  ring[g % RING][:, w:w + P], start=(f == 0), stop=(f == FC - 1))
                last.then_inc(down_done, 1)

            for g in range(LOTS + 2):
                if g < LOTS:
                    up(g)
                if 1 <= g <= LOTS:
                    turn_up(g - 1)
                if g >= 2:
                    down(g - 2)
            pe.wait_ge(pre_ready, LOTS)
            for n, dst in enumerate((kv, kps[0])):
                pe.wait_ge(down_copied, n + 1)
                for g in range(LOTS // 2):
                    last = turn(dst[:, g * P:(g + 1) * P], down_sb[:, n * (LOTS // 2) + g, :], ident[:, :])
            last.then_inc(ffn_turned, 1)
            pe.wait_ge(ffnt_ready, 1)
            for q in range(2):
                last = turn(ms[:, q * P:(q + 1) * P],
                            ffn_t[:, :, :].rearrange("p b e -> p (b e)")[:, q * P:(q + 1) * P], ident[:, :])
            last.then_inc(ffn_turned, 1)
            pe.wait_ge(ffno_ready, 1)
            for q in range(2):
                for k in range(TOPK):
                    last = mm(kps[q][:, k * P:(k + 1) * P], share[:, q, k * P:(k + 1) * P], ffn_o[:, q, :],
                              start=True, stop=True)
                last.then_inc(added_done, 1)


def kernel(**inputs):
    import numpy as np
    import concourse.bacc as bacc
    from concourse.bass_utils import run_bass_kernel_spmd

    a = {k: np.asarray(v) for k, v in inputs.items()}

    t = a["x"].reshape(2, 2, P, PAIR_UNITS, HALF // P, P).transpose(0, 3, 5, 1, 4, 2)
    x = np.ascontiguousarray(t).reshape(UNITS, P, GROUPS * P)

    c = np.empty((P, COLS), np.float32)
    parts = {
        "g0": np.broadcast_to(a["L0_conv_ln0_g"], (P, P)), "b0": np.broadcast_to(a["L0_conv_ln0_b"], (P, P)),
        "w_out": a["L0_conv_W_out"].T, "w_whiten": a["L0_conv_W_whiten"], "w_key": a["L0_conv_W_key"].T,
        "w_recep": a["L0_conv_W_recep"].T,
        "w_value": a["L0_conv_W_value"].T.reshape(CHUNKS, P, P).transpose(1, 0, 2).reshape(P, HID),
        "gate_w": a["L0_ffn_gate_w"].T, "g1": a["L0_conv_ln1_g"][:, None], "b1": a["L0_conv_ln1_b"][:, None],
        "g2": a["L0_conv_ln2_g"][:, None], "b2": a["L0_conv_ln2_b"][:, None],
        "gate_b": np.concatenate([a["L0_ffn_gate_b"]] * 2)[:, None],
        "ffn_b1": a["L0_ffn_weight1"][:, P, :].reshape(EXPERTS, FC, P).transpose(2, 0, 1).reshape(P, EXPERTS * FC),
        "ffn_b2": a["L0_ffn_weight2"][:, FFN, :].T,
    }
    for name, value in parts.items():
        c[:, COL[name][0]:COL[name][1]] = value

    w1 = a["L0_ffn_weight1"][:, :P, :].reshape(LOTS, FG, P, FFN).transpose(0, 2, 1, 3).reshape(LOTS, P, FG * FFN)
    w2 = a["L0_ffn_weight2"][:, :FFN, :].reshape(LOTS, FG, FC, P, P).transpose(0, 3, 1, 2, 4)
    wff = np.concatenate([w1, w2.reshape(LOTS, P, FG * FFN)], axis=2)

    nc = bacc.Bacc("TRN2", target_bir_lowering=False, num_devices=1)
    arrays = {"x_dram": x, "cst_dram": c, "wff_dram": np.ascontiguousarray(wff)}
    args = [nc.dram_tensor(n, v.shape, mybir.dt.from_np(v.dtype), kind="ExternalInput").ap() for n, v in arrays.items()]
    out = nc.dram_tensor("out_dram", x.shape, F32, kind="ExternalOutput").ap()
    metaformer_kernel(nc, *args, out)
    r = run_bass_kernel_spmd(nc, [arrays], core_ids=[0]).results[0]["out_dram"]
    y = np.asarray(r).reshape(2, PAIR_UNITS, P, 2, HALF // P, P).transpose(0, 3, 5, 1, 4, 2)
    return np.ascontiguousarray(y).reshape(BATCH, P, P, P)
```

```python
from contextlib import ExitStack

import concourse.bass as bass
from concourse import mybir

F32 = mybir.dt.float32
F32R = mybir.dt.float32r
U32 = mybir.dt.uint32
ALU = mybir.AluOpType
ACT = mybir.ActivationFunctionType
AX = mybir.AxisListType

P = 128
BATCH, TOKENS = 4, 128 * 128
HALF = 512
UNIT = 2 * HALF
GROUPS = UNIT // P
PAIR_UNITS = TOKENS // HALF
UNITS = BATCH // 2 * PAIR_UNITS
HID = 512
CHUNKS = HID // P
EXPERTS, TOPK, FFN = 64, 8, 512
FC = FFN // P
FG = 4
LOTS = EXPERTS // FG
LOT = FG * (FFN + FC * P)
RING = 7
RING_OWN = 3
CAND = PAIR_UNITS * TOPK

_at = 0
COL = {}
for _name, _n in (("g0", P), ("b0", P), ("w_out", P), ("w_whiten", P), ("w_key", HID), ("w_recep", P),
                  ("w_value", HID), ("gate_w", EXPERTS), ("g1", 1), ("b1", 1), ("g2", 1), ("b2", 1),
                  ("gate_b", 1), ("ffn_b1", EXPERTS * FC), ("ffn_b2", EXPERTS)):
    COL[_name] = (_at, _at + _n)
    _at += _n
COLS = _at

LN = {0: (1.0 + 1e-5, 1e-11), 1: (1.0, 4e-5), 2: (1.0, 4e-5), 3: (1.0, 1e-5)}
MEAN = {0: True, 1: True, 2: False, 3: False}
LN_STEPS = {0: 8, 1: 9, 2: 7, 3: 7}

UNROLL = 4
Z1_FIRST = 4
AHEAD, BEHIND = 4, 2
LOOPS = ((5, 7), (PAIR_UNITS + 1, 6))


def metaformer_kernel(nc, x, cst, wff, outs):
    ctx = ExitStack()
    with ctx:
        def sb(name, shape, dt=F32):
            return ctx.enter_context(nc.sbuf_tensor(name, shape, dt))

        def sem(name):
            return ctx.enter_context(nc.semaphore(name))

        C = sb("constants", [P, COLS])
        ident = sb("ident", [P, P])
        gb0 = sb("g0_b0_twice", [P, 2, P])
        w_kr = sb("w_key_recep", [P, HID + P])
        w_hi = sb("w_key_recep_hi", [P, HID + P], F32R)
        w_lo = sb("w_key_recep_lo", [P, HID + P], F32R)
        w_gate = sb("w_gate_centred", [P, EXPERTS])
        centre = sb("centre", [P, P])
        bias_kr = sb("bias_key_recep", [P, CHUNKS + 1])
        g_half = sb("minus_half", [P, 2 * TOPK])
        g_quarter = sb("quarter_scale", [P, 2, 2 * TOPK])

        def col(name):
            return C[:, COL[name][0]:COL[name][1]]

        xt = sb("x_tok", [P, 4, GROUPS, P])
        t0 = sb("t0_tok", [P, 2, GROUPS, P])
        z1 = sb("z1_tok", [P, GROUPS, P])
        t1 = sb("t1_tok", [P, GROUPS, P])
        res = sb("residual_tok", [P, 2, GROUPS, P])
        y2_hi = sb("y2_chan_hi", [P, 2, UNIT], F32R)
        y2_lo = sb("y2_chan_lo", [P, 2, UNIT], F32R)
        hid = sb("hidden", [P, CHUNKS, UNIT])
        x1 = sb("x1_tok", [P, 2, GROUPS, P])
        work = sb("work", [P, 2 * LOT])

        def tok(n):
            return work[:, n * UNIT:(n + 1) * UNIT].rearrange("p (g c) -> p g c", c=P)

        def chan(n):
            return work[:, n * UNIT:(n + 1) * UNIT]

        z0, z2, z3 = tok(0), tok(1), tok(2)
        y1, sl, gate_r, rk, tn = chan(3), chan(4), chan(5), chan(6), chan(7)
        lg = sb("logits", [P, HALF])
        ex = sb("exp_scratch", [P, HALF])
        st = [sb(f"stats{n}", [P, GROUPS, 6]) for n in range(4)]
        sm = [sb(f"sums{n}", [P, GROUPS, 2]) for n in range(4)]
        df = [sb(f"diffs{n}", [P, GROUPS]) for n in range(4)]
        va = [sb(f"var{n}", [P, GROUPS]) for n in range(4)]
        neg_mean = [sb(f"neg_mean{n}", [P, GROUPS]) for n in range(2)] + [None, None]
        shift1 = sb("shift1", [P, GROUPS])
        rstd = [sb(f"rstd{n}", [P, GROUPS]) for n in range(4)]

        mx = sb("unit_max8", [P, 2, TOPK])
        mi = sb("unit_index8", [P, 2, TOPK], U32)
        neg = sb("unit_neg_max", [P, 2])
        cval = sb("cand_values", [P, UNITS * TOPK])
        cidx = sb("cand_index", [P, UNITS * TOPK])
        csum = sb("unit_exp_sums", [P, UNITS])

        own = sb("expert_weights", [P, RING_OWN, LOT])
        ring = [(t[:, 0:LOT // 2], t[:, LOT // 2:LOT]) for t in
                [own[:, n, :] for n in range(RING_OWN)] + [hid[:, :, :].rearrange("p a n -> p (a n)")]]
        ring += [tuple(t.rearrange("p a g c -> p (a g c)") for t in (xt[:, 2:4, :, :], x1[:, :, :, :]))]
        ring += [(work[:, n * LOT:n * LOT + LOT // 2], work[:, n * LOT + LOT // 2:(n + 1) * LOT]) for n in range(2)]

        iota_i = sb("iota_int", [P, 2, CAND], mybir.dt.int32)
        iota_f = sb("iota_pos_tile", [P, 2, CAND])
        half_bit = sb("half_bit", [P, 2 * TOPK], U32)
        v8 = sb("top_values", [P, 2, TOPK])
        pos = sb("top_pos", [P, 2, TOPK], U32)
        posf = sb("top_pos_f", [P, 2, TOPK])
        seq = sb("top_token", [P, 2 * TOPK])
        rows_t = sb("row_parts", [P, 4, 2 * TOPK], U32)
        rows = sb("rows", [P, 2 * TOPK], U32)
        rowsf = sb("rows_f", [P, 2 * TOPK])
        neg_m = sb("neg_top", [P, 2])
        e_max = sb("exp_unit_max", [P, 2, PAIR_UNITS])
        den = sb("denominator", [P, 2])
        rden = sb("rdenominator", [P, 2])
        prob = sb("probs", [P, 2, TOPK])
        den_junk = sb("denominator_junk", [P, 2, PAIR_UNITS])
        g_st = [sb(f"g_stats{q}", [P, TOPK, 6]) for q in range(2)]
        g_sm = sb("g_sums", [P, 2, TOPK, 2])
        g_df = sb("g_diffs", [P, 2, TOPK])
        g_va = sb("g_var", [P, 2, TOPK])
        g_neg_mean = sb("g_mean", [P, 2, TOPK])
        g_rstd = sb("g_rstd", [P, 2, TOPK])
        weight = sb("pool_weights", [P, 2, TOPK])
        shift_junk = sb("pool_shift_junk", [P, 2, TOPK])
        shift = sb("pool_shift", [P, 2])
        pooled = sb("pooled", [P, 2, 2, P])
        pooled_t = sb("pooled_chan", [P, BATCH, EXPERTS])
        hpre = sb("expert_pre", [P, 2, FC * FG * BATCH])
        hact = sb("expert_hidden", [P, 2, FC * FG * BATCH])
        ffn_t = sb("expert_out_chan", [P, BATCH, EXPERTS])
        ffn_o = sb("expert_out", [P, 2, P])
        junk = t0[:, :, :, :].rearrange("p a g c -> p (a g c)")
        picked = xt[:, 0:2, :, :].rearrange("p a g c -> p (a g) c")
        row_b = res[:, :, :, :].rearrange("p a g c -> p (a g) c")
        row_all = t0[:, :, :, :].rearrange("p a g c -> p a (g c)")
        share = res[:, :, :, :].rearrange("p a g c -> p a (g c)")
        part = t1[:, :, :].rearrange("p g c -> p (g c)")
        up_sb = z1[:, :, :].rearrange("p (a g) c -> p a (g c)", a=2)
        down_sb = [z1, t1]
        final = res[:, :, :, :].rearrange("p a g c -> p (a g) c")

        kps = [ctx.enter_context(nc.psum_tensor(f"key{n}", [P, UNIT], F32)) for n in range(2)]
        kv = ctx.enter_context(nc.psum_tensor("kv", [P, UNIT], F32))
        ms = ctx.enter_context(nc.psum_tensor("misc", [P, UNIT], F32))

        cst_loaded = sem("cst_loaded")
        x_loaded = [sem(f"x_loaded{n}") for n in range(4)]
        x1_stored = [sem("x1_stored0"), sem("x1_stored1")]
        lot_loaded = [[sem(f"weight{w}_loaded{n}") for w in (1, 2)] for n in range(RING)]
        pool_const = sem("pool_const")
        fold_mm, fold_raw, fold_bias, fold_ready = sem("fold_mm"), sem("fold_raw"), sem("fold_bias"), sem("fold_ready")
        iota_ready = sem("iota_ready")
        stats_ready = [sem(f"stats_ready{n}") for n in range(4)]
        ln_steps = [sem(f"ln_steps{n}") for n in range(4)]
        z_ready = [sem(f"z_ready{n}") for n in range(4)]
        t0_steps = sem("t0_steps")
        z1_turned, y1_ready, tanh_ready, silu_ready = sem("z1_turned"), sem("y1_ready"), sem("tanh_ready"), sem("silu_ready")
        att_done, t1_ready, res_ready = sem("att_done"), sem("t1_ready"), sem("res_ready")
        z2_turned, y2_ready, y2_lo_ready = sem("z2_turned"), sem("y2_ready"), sem("y2_lo_ready")
        fold_centre, fold_mm2, fold_lo = sem("fold_centre"), sem("fold_mm2"), sem("fold_lo")
        up_copied, up_turned, down_copied = sem("up_copied"), sem("up_turned"), sem("down_copied")
        recep_done, recep_ready = sem("recep_done"), sem("recep_ready")
        key_done, relu_done, value_done = sem("key_done"), sem("relu_done"), sem("value_done")
        sq_done = sem("sq_done")
        rk_ready, rk_turned, x1_ready = sem("rk_ready"), sem("rk_turned"), sem("x1_ready")
        z3_turned, tn_ready = sem("z3_turned"), sem("tn_ready")
        gate_done, lg_ready = sem("gate_done"), sem("lg_ready")
        max_ready, index_ready, neg_ready, exp_ready, cand_kept = (
            sem("max_ready"), sem("index_ready"), sem("neg_ready"), sem("exp_ready"), sem("cand_kept"))
        pick, negm_ready, emax_ready = sem("pick"), sem("negm_ready"), sem("emax_ready")
        rows_ready, gathered = sem("rows_ready"), [sem(f"gathered{k}") for k in range(TOPK)]
        scattered = [sem(f"scattered{q}") for q in range(2)]
        g_stats_ready, g_ln, pooling, pool_turned = sem("g_stats_ready"), sem("g_ln"), sem("pooling"), sem("pool_turned")
        pooled_ready, up_done, pre_ready, gelu_ready, down_done = (
            sem("pooled_ready"), sem("up_done"), sem("pre_ready"), sem("gelu_ready"), sem("down_done"))
        rowb_ready, row_turned, row_copied = sem("rowb_ready"), sem("row_turned"), sem("row_copied")
        ffnt_ready, ffn_turned, ffno_ready, added_done, final_ready = (
            sem("ffnt_ready"), sem("ffn_turned"), sem("ffno_ready"), sem("added_done"), sem("final_ready"))

        def at(u, d):
            return (u[0] + d, u[1])

        def num(u):
            return u[0] if u[1] is None else u[1] * UNROLL + u[0]

        def real(u):
            return u[1] is not None or 0 <= u[0] < UNITS

        def wait(eng, s, u, per=1, k=None):
            v = per * u[0] + (per if k is None else k)
            if u[1] is not None:
                eng.wait_ge(s, u[1] * (UNROLL * per) + v)
            elif v > 0:
                eng.wait_ge(s, v)

        def wait_dma(eng, s, u, n):
            v = 16 * (u[0] // n + 1)
            if u[1] is not None:
                eng.wait_ge(s, u[1] * (16 * UNROLL // n) + v)
            elif v > 0:
                eng.wait_ge(s, v)

        def run_steps(eng, step, between={}):
            def peeled(numbers):
                for i in numbers:
                    step((i, None))
                    if i in between:
                        between[i]()

            done = -AHEAD
            for first, turns in LOOPS:
                peeled(range(done, first))
                with eng.Fori(0, turns) as j:
                    for n in range(UNROLL):
                        step((first + n, j))
                done = first + UNROLL * turns
            peeled(range(done, UNITS + BEHIND))

        block = ctx.enter_context(nc.Block())

        @block.sync
        def _(sp):
            def load_x(u):
                if real(u):
                    wait(sp, res_ready, at(u, -4))
                    sp.dma_start(xt[:, u[0] % 4, :, :].rearrange("p g c -> p (g c)"),
                                 x[bass.ds(num(u), 1), :, :].rearrange("a p n -> (a p) n")
                                 ).then_inc(x_loaded[u[0] % 4], 16)

            def step(i):
                b = at(i, -1)
                if real(b):
                    wait(sp, x1_ready, b, 2)
                    q = int(b[0] >= PAIR_UNITS)
                    sp.dma_start(outs[q][bass.ds(num(at(b, -q * PAIR_UNITS)), 1), :, :].rearrange("a p n -> (a p) n"),
                                 x1[:, b[0] % 2, :, :].rearrange("p g c -> p (g c)")
                                 ).then_inc(x1_stored[b[0] % 2], 16)
                load_x(at(i, 5))

            load_x((0, None))
            sp.dma_start(C[:, :], cst[:, :]).then_inc(cst_loaded, 16)

            def load_weight(g, n):
                sp.dma_start(ring[g % RING][n], wff[g, :, n * (LOT // 2):(n + 1) * (LOT // 2)]
                             ).then_inc(lot_loaded[g % RING][n], 16)

            def load_lot(g):
                load_weight(g, 0)
                load_weight(g, 1)

            def load_first():
                for g in range(RING_OWN):
                    load_lot(g)

            def load_hidden():
                sp.wait_ge(value_done, UNITS * CHUNKS)
                load_lot(RING_OWN)

            run_steps(sp, step, {0: load_first, UNITS: load_hidden})
            for par in range(2):
                sp.wait_ge(x1_stored[par], 16 * (UNITS // 2))
            sp.wait_ge(z_ready[3], UNITS)
            sp.wait_ge(res_ready, UNITS)
            load_lot(RING_OWN + 1)
            sp.wait_ge(z3_turned, UNITS)
            load_lot(RING_OWN + 2)
            sp.wait_ge(gate_done, UNITS)
            for k in range(TOPK):
                sp.wait_ge(gathered[k], 16 * 2)
            for g in range(RING_OWN + 3, RING):
                load_lot(g)
            for g in range(RING, LOTS + 1):
                if g < LOTS:
                    sp.wait_ge(up_done, g - RING + 1)
                    load_weight(g, 0)
                if g > RING:
                    sp.wait_ge(down_done, g - RING)
                    load_weight(g - 1, 1)

        def ln_on_pool(pool, s, base, stat, sums, diff, var, neg_mu, shift, rs, exponent, quarter, scale, eps):
            tt, ts = nc.gpsimd.tensor_tensor, nc.gpsimd.tensor_scalar
            n = 5
            tt(out=sums, in0=stat[:, :, 1:3], in1=stat[:, :, 4:6], op=ALU.add).then_inc(s, 1)
            tt(out=diff, in0=stat[:, :, 1], in1=stat[:, :, 4], op=ALU.subtract).then_inc(s, 1)
            base(2)
            tt(out=diff, in0=diff, in1=diff, op=ALU.mult).then_inc(s, 1)
            ts(var, sums[:, :, 1], scale / P, eps, ALU.mult, ALU.add).then_inc(s, 1)
            if neg_mu is not None:
                ts(neg_mu, sums[:, :, 0], -0.5, None, ALU.mult).then_inc(s, 1)
                n = 6
            base(3)
            tt(out=diff, in0=diff, in1=quarter, op=ALU.mult).then_inc(s, 1)
            base(n)
            tt(out=var, in0=var, in1=diff, op=ALU.add).then_inc(s, 1)
            base(n + 1)
            tt(out=rs, in0=var, in1=exponent, op=ALU.pow).then_inc(s, 1)
            if shift is not None:
                base(n + 2)
                tt(out=shift, in0=neg_mu, in1=rs, op=ALU.mult).then_inc(s, 1)

        @block.gpsimd
        def _(pool):
            def ln(n, u):
                wait(pool, stats_ready[n], u)
                wait(pool, z_ready[n], at(u, -1))
                ln_on_pool(pool, ln_steps[n], lambda k: wait(pool, ln_steps[n], u, LN_STEPS[n], k),
                           st[n][:, :, :], sm[n][:, :, :], df[n][:, :], va[n][:, :],
                           neg_mean[n][:, :] if MEAN[n] else None, shift1[:, :] if n == 1 else None, rstd[n][:, :],
                           g_half[:, 0:GROUPS], g_quarter[:, min(n, 1), 0:GROUPS], *LN[n])

            def step(i):
                d, a, f, e, b, c = at(i, 4), at(i, 3), at(i, 2), at(i, 1), at(i, -1), at(i, -2)
                if real(a):
                    wait(pool, z_ready[0], a)
                    wait(pool, t1_ready, at(a, -2), 2)
                    nc.gpsimd.tensor_tensor(out=z0, in0=z0, in1=gb0[:, 0:1, :].to_broadcast([P, GROUPS, P]),
                                            op=ALU.mult).then_inc(t0_steps, 1)
                    wait(pool, t0_steps, a, 2, 1)
                    nc.gpsimd.tensor_tensor(out=t0[:, a[0] % 2, :, :], in0=z0,
                                            in1=gb0[:, 1:2, :].to_broadcast([P, GROUPS, P]),
                                            op=ALU.add).then_inc(t0_steps, 1)
                if real(b):
                    ln(3, b)
                if real(a):
                    ln(1, a)
                if real(e):
                    wait(pool, t1_ready, e, 2)
                    wait(pool, x1_ready, at(e, -2), 2)
                    nc.gpsimd.tensor_tensor(out=res[:, e[0] % 2, :, :], in0=t1[:, :, :], in1=xt[:, e[0] % 4, :, :],
                                            op=ALU.add).then_inc(res_ready, 1)
                if real(d):
                    ln(0, d)
                if real(f):
                    ln(2, f)
                if i == (UNITS - 1, None):
                    gather(0)
                if real(c):
                    wait(pool, index_ready, c)
                    v = num(c) * TOPK
                    nc.gpsimd.tensor_copy(cval[:, bass.ds(v, TOPK)], mx[:, c[0] % 2, :]).then_inc(cand_kept, 1)
                    nc.gpsimd.tensor_copy(cidx[:, bass.ds(v, TOPK)], mi[:, c[0] % 2, :]).then_inc(cand_kept, 1)

            nc.gpsimd.memset(ident[:, :], 0.0).then_inc(pool_const, 1)
            nc.gpsimd.memset(g_half[:, :], -0.5).then_inc(pool_const, 1)
            for n in range(2):
                nc.gpsimd.memset(g_quarter[:, n, :], LN[n][0] / 4).then_inc(pool_const, 1)
            pool.wait_ge(pool_const, 4)
            nc.gpsimd.affine_select(out=ident[:, :], in_=ident[:, :], compare_op=ALU.not_equal, fill=1.0, base=0,
                                    pattern=[[-1, P]], channel_multiplier=1).then_inc(pool_const, 1)
            nc.gpsimd.iota(iota_i[:, 0, :], pattern=[[1, CAND]], base=0, channel_multiplier=0).then_inc(pool_const, 1)
            nc.gpsimd.iota(iota_i[:, 1, :], pattern=[[HALF, PAIR_UNITS], [0, TOPK]], base=0,
                           channel_multiplier=0).then_inc(pool_const, 1)
            nc.gpsimd.iota(half_bit[:, :], pattern=[[0, 2 * TOPK]], base=0, channel_multiplier=1).then_inc(pool_const, 1)
            pool.wait_ge(pool_const, 8)
            nc.gpsimd.tensor_copy(iota_f[:, :, :], iota_i[:, :, :]).then_inc(iota_ready, 1)
            pool.wait_ge(fold_ready, 1)

            def rows_of(q):
                return outs[q].rearrange("u p (g c) -> (u p g) c", c=P)

            def row_index(q, k):
                return bass.IndirectOffsetOnAxis(ap=rows[:, q * TOPK + k:q * TOPK + k + 1], axis=0)

            def gather(q):
                for par in range(2):
                    pool.wait_ge(x1_stored[par], 16 * (PAIR_UNITS // 2) * (q + 1))
                pool.wait_ge(rows_ready, q + 1)
                pool.wait_ge(res_ready, UNITS - 2)
                for k in range(TOPK):
                    nc.gpsimd.indirect_dma_start(out=picked[:, q * TOPK + k, :], out_offset=None, in_=rows_of(q),
                                                 in_offset=row_index(q, k)).then_inc(gathered[k], 16)

            def picked_ln(q):
                pool.wait_ge(g_stats_ready, q + 1)
                ln_on_pool(pool, g_ln, lambda k: pool.wait_ge(g_ln, q * LN_STEPS[0] + k), g_st[q][:, :, :],
                           g_sm[:, q, :, :], g_df[:, q, :], g_va[:, q, :], g_neg_mean[:, q, :], None, g_rstd[:, q, :],
                           g_half[:, 0:TOPK], g_quarter[:, 1, 0:TOPK], *LN[3])

            run_steps(pool, step, {UNITS: lambda: picked_ln(0)})
            gather(1)
            picked_ln(1)
            for q in range(2):
                pool.wait_ge(final_ready, q + 1)
            for k in range(TOPK):
                for q in range(2):
                    if k:
                        pool.wait_ge(scattered[q], 16 * k)
                    nc.gpsimd.indirect_dma_start(out=rows_of(q), out_offset=row_index(q, k),
                                                 in_=final[:, q * TOPK + k, :], in_offset=None).then_inc(scattered[q], 16)
            for q in range(2):
                pool.wait_ge(scattered[q], 16 * TOPK)

        @block.scalar
        def _(act):
            def relu(i, ch):
                wait(act, key_done, i, CHUNKS, ch + 1)
                wait(act, value_done, at(i, -1), CHUNKS, ch + 1)
                nc.scalar.activation(hid[:, ch, :], kps[ch % 2][:, :], ACT.Relu,
                                     bias=bias_kr[:, ch:ch + 1]).then_inc(relu_done, 1)

            def square(i, ch):
                wait(act, relu_done, i, CHUNKS, ch + 1)
                nc.scalar.activation(hid[:, ch, :], hid[:, ch, :], ACT.Square).then_inc(sq_done, 1)

            def scale_z1(u, groups):
                for g in groups:
                    last = nc.scalar.activation(z1[:, g, :], t0[:, u[0] % 2, g, :], ACT.Identity,
                                                bias=shift1[:, g:g + 1], scale=rstd[1][:, g:g + 1])
                if g == GROUPS - 1:
                    last.then_inc(z_ready[1], 1)

            def step(i):
                a, f, e, c = at(i, 3), at(i, 2), at(i, 1), at(i, -2)
                if real(c):
                    wait(act, z3_turned, c)
                    wait(act, gate_done, at(c, -1))
                    nc.scalar.activation(tn, ms[:, :], ACT.Copy).then_inc(tn_ready, 1)
                if real(i):
                    relu(i, 1)
                if real(i):
                    square(i, 1)
                if real(f):
                    scale_z1(f, range(Z1_FIRST, GROUPS))
                if real(i):
                    relu(i, 2)
                    square(i, 2)
                if real(e):
                    wait(act, z2_turned, e)
                    wait(act, recep_done, at(e, -2), 2)
                    wait(act, key_done, at(e, -2), CHUNKS)
                    for h in range(2):
                        w = slice(h * HALF, (h + 1) * HALF)
                        nc.scalar.activation(y2_hi[:, e[0] % 2, w], ms[:, w], ACT.Copy).then_inc(y2_ready, 1)
                if real(i):
                    relu(i, 3)
                if real(i):
                    square(i, 3)
                if real(f):
                    wait(act, z1_turned, f)
                    wait(act, silu_ready, at(f, -1))
                    nc.scalar.activation(y1, ms[:, :], ACT.Identity, bias=col("b1"),
                                         scale=col("g1")).then_inc(y1_ready, 1)
                if real(f):
                    wait(act, y1_ready, f)
                    wait(act, att_done, at(f, -1), 2)
                    nc.scalar.activation(sl, y1, ACT.Tanh, scale=0.5).then_inc(tanh_ready, 1)
                if real(c):
                    wait(act, gate_done, c)
                    wait(act, index_ready, at(c, -1))
                    wait(act, exp_ready, at(c, -1))
                    nc.scalar.activation(lg[:, :], ms[:, 0:HALF], ACT.Identity,
                                         bias=col("gate_b")).then_inc(lg_ready, 1)
                if real(i):
                    wait(act, rk_ready, at(i, -1))
                    for n, h in enumerate((1, 0)):
                        wait(act, recep_done, i, 2, n + 1)
                        nc.scalar.activation(gate_r[:, h * HALF:(h + 1) * HALF], ms[:, h * HALF:(h + 1) * HALF],
                                             ACT.Tanh, bias=bias_kr[:, CHUNKS:CHUNKS + 1],
                                             scale=0.5).then_inc(recep_ready, 1)
                if real(e):
                    relu(e, 0)
                    square(e, 0)
                if real(c):
                    wait(act, neg_ready, c)
                    nc.scalar.activation(ex[:, :], lg[:, :], ACT.Exp, bias=neg[:, c[0] % 2:c[0] % 2 + 1],
                                         accum_out=csum[:, bass.ds(num(c), 1)]).then_inc(exp_ready, 1)
                if real(a):
                    wait(act, z1_turned, at(a, -1))
                    wait(act, ln_steps[1], a, LN_STEPS[1])
                    scale_z1(a, range(Z1_FIRST))

            act.wait_ge(cst_loaded, 16)
            nc.scalar.activation(gb0[:, :, :].rearrange("p a c -> p (a c)"), C[:, COL["g0"][0]:COL["b0"][1]], ACT.Copy,
                                 scale=2.0).then_inc(fold_ready, 1)
            act.wait_ge(fold_mm, 1)
            nc.scalar.activation(hid[:, 0, 0:HID], kps[0][:, 0:HID], ACT.Copy).then_inc(fold_raw, 1)
            nc.scalar.activation(hid[:, 0, HID:HID + P], kps[0][:, HID:HID + P], ACT.Copy).then_inc(fold_raw, 1)
            nc.scalar.activation(hid[:, 1, 0:HID + P], kps[0][:, 0:HID + P], ACT.Identity,
                                 scale=col("g2")).then_inc(fold_raw, 1)
            act.wait_ge(fold_bias, 1)
            nc.scalar.activation(bias_kr[:, 0:CHUNKS], ms[:, 0:CHUNKS], ACT.Copy).then_inc(fold_ready, 1)
            nc.scalar.activation(bias_kr[:, CHUNKS:CHUNKS + 1], ms[:, CHUNKS:CHUNKS + 1], ACT.Copy,
                                 scale=0.5).then_inc(fold_ready, 1)
            act.wait_ge(fold_mm2, 1)
            nc.scalar.activation(w_kr[:, :], kps[1][:, 0:HID + P], ACT.Copy).then_inc(fold_ready, 1)
            nc.scalar.activation(w_hi[:, :], kps[1][:, 0:HID + P], ACT.Copy).then_inc(fold_ready, 1)
            nc.scalar.activation(w_gate[:, :], kv[:, 0:EXPERTS], ACT.Copy).then_inc(fold_ready, 1)
            act.wait_ge(fold_ready, 6)

            def top_exp(q):
                act.wait_ge(cand_kept, 2 * PAIR_UNITS * (q + 1))
                act.wait_ge(negm_ready, q + 1)
                nc.scalar.activation(
                    e_max[:, q, :], cval[:, q * CAND:(q + 1) * CAND].rearrange("p (u k) -> p u k", k=TOPK)[:, :, 0],
                    ACT.Exp, bias=neg_m[:, q:q + 1]).then_inc(emax_ready, 1)
                nc.scalar.activation(prob[:, q, :], v8[:, q, :], ACT.Exp, bias=neg_m[:, q:q + 1]).then_inc(emax_ready, 1)

            run_steps(act, step, {UNITS - 2: lambda: top_exp(0)})
            top_exp(1)
            for q in range(2):
                act.wait_ge(row_turned, q + 1)
                nc.scalar.activation(row_all[:, q, :], kps[q][:, :], ACT.Copy).then_inc(row_copied, 1)

            def copy_up(g):
                act.wait_ge(up_done, g + 1)
                if g >= 2:
                    act.wait_ge(up_turned, g - 1)
                nc.scalar.activation(up_sb[:, g % 2, :], kv[:, HALF * (g % 2):HALF * (g % 2 + 1)],
                                     ACT.Copy).then_inc(up_copied, 1)

            copy_up(0)
            for g in range(LOTS):
                if g + 1 < LOTS:
                    copy_up(g + 1)
                act.wait_ge(pre_ready, g + 1)
                if g >= 2:
                    act.wait_ge(down_done, g - 1)
                nc.scalar.activation(hact[:, g % 2, :], hpre[:, g % 2, :], ACT.Gelu).then_inc(gelu_ready, 1)

        @block.vector
        def _(dve):
            ts, tt, stt = nc.vector.tensor_scalar, nc.vector.tensor_tensor, nc.vector.scalar_tensor_tensor

            def half(t, h):
                return t[:, h * (GROUPS // 2):(h + 1) * (GROUPS // 2), :]

            def stats(n, src, source_ready=None, halves=(0, 1)):
                for k, h in enumerate(halves):
                    if source_ready:
                        source_ready(k + 1)
                    for g in range(h * GROUPS // 2, (h + 1) * GROUPS // 2):
                        last = nc.vector.bn_stats(st[n][:, g, :], src[:, g, :])
                last.then_inc(stats_ready[n], 1)

            def scale_rows(n, dst, src, u):
                wait(dve, ln_steps[n], u, LN_STEPS[n])
                tt(dst, src, rstd[n][:, :, None].to_broadcast([P, GROUPS, P]),
                   ALU.mult).then_inc(z_ready[n], 1)

            def flat(t):
                return t.rearrange("p g c -> p (g c)")

            def silu(f):
                wait(dve, tanh_ready, f)
                stt(out=sl, in0=sl, scalar=1.0, in1=y1, op0=ALU.add, op1=ALU.mult).then_inc(silu_ready, 1)

            def step(i):
                d, a, f, e, b, c = at(i, 4), at(i, 3), at(i, 2), at(i, 1), at(i, -1), at(i, -2)
                if real(f) and not real(e):
                    silu(f)
                if real(b):
                    wait(dve, rk_turned, b)
                    wait_dma(dve, x1_stored[b[0] % 2], at(b, -2), 2)
                    for h in range(2):
                        tt(flat(half(x1[:, b[0] % 2, :, :], h)), flat(half(res[:, b[0] % 2, :, :], h)),
                           ms[:, h * HALF:(h + 1) * HALF], ALU.add).then_inc(x1_ready, 1)
                if real(e):
                    wait(dve, z2_turned, at(e, -1))
                    scale_rows(2, z2, t1[:, :, :], e)
                if real(b):
                    stats(3, x1[:, b[0] % 2, :, :], lambda k: wait(dve, x1_ready, b, 2, k))
                if real(e):
                    wait(dve, recep_done, at(e, -2), 2)
                    for h in range(2):
                        wait(dve, y2_ready, e, 2, h + 1)
                        w = slice(h * HALF, (h + 1) * HALF)
                        tt(y2_lo[:, e[0] % 2, w], ms[:, w], y2_hi[:, e[0] % 2, w].bitcast(F32),
                           ALU.subtract).then_inc(y2_lo_ready, 1)
                if real(a):
                    wait(dve, t0_steps, a, 2)
                    stats(1, t0[:, a[0] % 2, :, :])
                if real(b):
                    wait(dve, z3_turned, at(b, -1))
                    scale_rows(3, z3, x1[:, b[0] % 2, :, :], b)
                if real(d):
                    wait_dma(dve, x_loaded[d[0] % 4], d, 4)
                    stats(0, xt[:, d[0] % 4, :, :])
                if real(c):
                    wait(dve, cand_kept, at(c, -2), 2)
                    wait(dve, exp_ready, at(c, -2))
                    wait(dve, lg_ready, c)
                if real(f) and real(e):
                    silu(f)
                if real(c):
                    nc.vector.max(mx[:, c[0] % 2, :], lg[:, :]).then_inc(max_ready, 1)
                    wait(dve, max_ready, c)
                    ts(neg[:, c[0] % 2:c[0] % 2 + 1], mx[:, c[0] % 2, 0:1], -1.0, None, ALU.mult).then_inc(neg_ready, 1)
                if real(i):
                    wait(dve, value_done, i, CHUNKS)
                    wait(dve, recep_ready, i, 2)
                    wait(dve, rk_turned, at(i, -1))
                    stt(out=rk, in0=gate_r, scalar=1.0, in1=kv[:, :], op0=ALU.add,
                        op1=ALU.mult).then_inc(rk_ready, 1)
                if real(f):
                    wait(dve, res_ready, at(f, -1))
                    for n, h in enumerate((1, 0)):
                        wait(dve, att_done, f, 2, n + 1)
                        tt(flat(half(t1[:, :, :], h)), flat(half(t0[:, f[0] % 2, :, :], h)),
                           ms[:, h * HALF:(h + 1) * HALF], ALU.add).then_inc(t1_ready, 1)
                    stats(2, t1, lambda k: wait(dve, t1_ready, f, 2, k), (1, 0))
                if real(c):
                    nc.vector.max_index(mi[:, c[0] % 2, :], mx[:, c[0] % 2, :], lg[:, :]).then_inc(index_ready, 1)
                if real(d):
                    wait(dve, ln_steps[0], d, LN_STEPS[0])
                    wait(dve, t0_steps, a, 2)
                    for g in range(GROUPS):
                        last = ts(z0[:, g, :], xt[:, d[0] % 4, g, :], neg_mean[0][:, g:g + 1],
                                  rstd[0][:, g:g + 1], ALU.add, ALU.mult)
                    last.then_inc(z_ready[0], 1)

            dve.wait_ge(pool_const, 5)
            ts(centre[:, :], ident[:, :], -1.0 / P, None, ALU.add).then_inc(fold_centre, 1)

            def split_weights():
                dve.wait_ge(fold_ready, 5)
                tt(w_lo[:, :], w_kr[:, :], w_hi[:, :].bitcast(F32), ALU.subtract).then_inc(fold_lo, 1)

            count = [0]

            def then(ins):
                count[0] += 1
                ins.then_inc(pick, 1)
                dve.wait_ge(pick, count[0])

            def find(q):
                dve.wait_ge(cand_kept, 2 * PAIR_UNITS * (q + 1))
                if q == 0:
                    dve.wait_ge(iota_ready, 1)
                    then(ts(half_bit[:, :], half_bit[:, :], 6, 2, ALU.logical_shift_right, ALU.logical_shift_left))
                vals, idxs = (t[:, q * CAND:(q + 1) * CAND] for t in (cval, cidx))
                then(nc.vector.max(v8[:, q, :], vals))
                ts(neg_m[:, q:q + 1], v8[:, q, 0:1], -1.0, None, ALU.mult).then_inc(negm_ready, 1)
                tt(idxs, idxs, iota_f[:, 1, :], ALU.add)
                then(nc.vector.max_index(pos[:, q, :], v8[:, q, :], vals))
                then(nc.vector.tensor_copy(posf[:, q, :], pos[:, q, :]))

            def locate(q):
                w = slice(q * TOPK, (q + 1) * TOPK)
                idxs = cidx[:, q * CAND:(q + 1) * CAND]
                for k in range(TOPK):
                    last = stt(out=junk[:, k * CAND:(k + 1) * CAND], in0=iota_f[:, 0, :], scalar=posf[:, q, k:k + 1],
                               in1=idxs, op0=ALU.is_equal, op1=ALU.mult, accum_out=seq[:, q * TOPK + k:q * TOPK + k + 1])
                then(last)
                r = [rows_t[:, n, w] for n in range(4)]
                then(nc.vector.tensor_copy(r[0], seq[:, w]))
                ts(r[1], r[0], 9, 10, ALU.logical_shift_right, ALU.logical_shift_left)
                ts(r[2], r[0], P - 1, 3, ALU.bitwise_and, ALU.logical_shift_left)
                then(ts(r[3], r[0], 7, 3, ALU.logical_shift_right, ALU.bitwise_and))
                tt(r[1], r[1], r[2], ALU.bitwise_or)
                then(tt(r[3], r[3], half_bit[:, w], ALU.bitwise_or))
                tt(rows[:, w], r[1], r[3], ALU.bitwise_or).then_inc(rows_ready, 1)

            def softmax(q):
                dve.wait_ge(exp_ready, PAIR_UNITS * (q + 1))
                dve.wait_ge(emax_ready, 2 * q + 2)
                then(stt(out=den_junk[:, q, :], in0=e_max[:, q, :], scalar=1.0,
                         in1=csum[:, q * PAIR_UNITS:(q + 1) * PAIR_UNITS], op0=ALU.mult, op1=ALU.mult,
                         accum_out=den[:, q:q + 1]))
                then(nc.vector.reciprocal(rden[:, q:q + 1], den[:, q:q + 1]))
                then(ts(prob[:, q, :], prob[:, q, :], rden[:, q:q + 1], None, ALU.mult))

            def picked_stats(q):
                for k in range(TOPK):
                    dve.wait_ge(gathered[k], 16 * (q + 1))
                    last = nc.vector.bn_stats(g_st[q][:, k, :], picked[:, q * TOPK + k, :])
                last.then_inc(g_stats_ready, 1)

            def pool_picked(q):
                dve.wait_ge(g_ln, (q + 1) * LN_STEPS[0])
                then(tt(weight[:, q, :], prob[:, q, :], g_rstd[:, q, :], ALU.mult))
                then(stt(out=shift_junk[:, q, :], in0=weight[:, q, :], scalar=1.0, in1=g_neg_mean[:, q, :],
                         op0=ALU.mult, op1=ALU.mult, accum_out=shift[:, q:q + 1]))
                for k in range(TOPK):
                    row, wk = picked[:, q * TOPK + k, :], weight[:, q, k:k + 1]
                    dst = pooled[:, q, k % 2, :]
                    if k == 0:
                        last = ts(dst, row, wk, shift[:, q:q + 1], ALU.mult, ALU.add)
                    elif k == 1:
                        last = ts(dst, row, wk, None, ALU.mult)
                    else:
                        last = stt(out=dst, in0=row, scalar=wk, in1=dst, op0=ALU.mult, op1=ALU.add)
                    if k % 2:
                        then(last)
                tt(pooled[:, q, 0, :], pooled[:, q, 0, :], pooled[:, q, 1, :], ALU.add).then_inc(pooling, 1)

            run_steps(dve, step, {-AHEAD: split_weights, UNITS - 3: lambda: find(0), UNITS - 2: lambda: locate(0),
                                  UNITS - 1: lambda: softmax(0), UNITS: lambda: picked_stats(0)})
            find(1)
            locate(1)
            softmax(1)
            dve.wait_ge(rows_ready, 2)
            then(nc.vector.tensor_copy(rowsf[:, :], rows[:, :]))
            for n in range(2 * TOPK):
                last = nc.vector.tensor_copy(row_b[:, n, :], rowsf[:, n:n + 1].to_broadcast([P, P]))
            last.then_inc(rowb_ready, 1)
            pool_picked(0)
            picked_stats(1)
            pool_picked(1)
            dve.wait_ge(pool_turned, 1)
            nc.vector.tensor_copy(pooled_t[:, :, :].rearrange("p b e -> p (b e)"), ms[:, 0:2 * P]).then_inc(pooled_ready, 1)

            def add_share(q, k):
                if k == 0:
                    dve.wait_ge(row_copied, q + 1)
                dst = part if k else share[:, q, :]
                then(ts(dst, row_all[:, q, :], rowsf[:, q * TOPK + k:q * TOPK + k + 1], prob[:, q, k:k + 1],
                        ALU.is_equal, ALU.mult))
                if k:
                    then(tt(share[:, q, :], share[:, q, :], part, ALU.add))

            b1 = col("ffn_b1").rearrange("p (g e f) -> p g f e", g=LOTS, e=FG)
            for g in range(LOTS):
                add_share(g // TOPK, g % TOPK)
                dve.wait_ge(up_turned, g + 1)
                if g >= 2:
                    dve.wait_ge(gelu_ready, g - 1)
                tt(hpre[:, g % 2, :].rearrange("p (f e b) -> p f e b", f=FC, e=FG),
                   kps[0][:, HALF * (g % 2):HALF * (g % 2 + 1)].rearrange("p (f e r) -> p f e r", f=FC, e=FG)[:, :, :, 0:BATCH],
                   b1[:, g, :, :][:, :, :, None].to_broadcast([P, FC, FG, BATCH]), ALU.add).then_inc(pre_ready, 1)
            half = LOTS // 2
            for n, src in enumerate((kps[1], ms)):
                dve.wait_ge(down_done, half * (n + 1))
                nc.vector.tensor_copy(flat(down_sb[n][:, :, :]),
                                      src[:, :]).then_inc(down_copied, 1)
            dve.wait_ge(ffn_turned, 1)
            for n, src in enumerate((kv, kps[0])):
                for b in range(BATCH):
                    last = tt(ffn_t[:, b, n * half * FG:(n + 1) * half * FG].rearrange("p (g e) -> p g e", e=FG),
                              src[:, :].rearrange("p (g e r) -> p g e r", e=FG, r=32)[:, :, :, b],
                              col("ffn_b2")[:, n * half * FG:(n + 1) * half * FG].rearrange("p (g e) -> p g e", e=FG),
                              ALU.add)
            last.then_inc(ffnt_ready, 1)
            dve.wait_ge(ffn_turned, 2)
            nc.vector.tensor_copy(ffn_o[:, :, :].rearrange("p q c -> p (q c)"), ms[:, 0:2 * P]).then_inc(ffno_ready, 1)
            for q in range(2):
                dve.wait_ge(added_done, q + 1)
                tt(final[:, q * TOPK:(q + 1) * TOPK, :].rearrange("p k c -> p (k c)"),
                   picked[:, q * TOPK:(q + 1) * TOPK, :].rearrange("p k c -> p (k c)"), kps[q][:, :],
                   ALU.add).then_inc(final_ready, 1)

        @block.tensor
        def _(pe):
            mm, turn = nc.tensor.matmul, nc.tensor.transpose

            def wait_first(h, *turns):
                for s, u in turns:
                    if real(u):
                        if s in (recep_ready, t1_ready):
                            wait(pe, s, u, 2, 2 - h)
                        elif s in (x1_ready, y2_lo_ready):
                            wait(pe, s, u, 2, h + 1)
                        else:
                            wait(pe, s, u)
                        return

            def turn_all(src, done, *turns, halves=(0, 1)):
                for h in halves:
                    wait_first(h, *turns)
                    for g in range(h * GROUPS // 2, (h + 1) * GROUPS // 2):
                        last = turn(ms[:, g * P:(g + 1) * P], src(g), ident[:, :])
                last.then_inc(done, 1)

            def project(dst, i, w, first, halves=(0, 1)):
                for h in halves:
                    for n, (wt, y) in enumerate(((w_hi, y2_hi), (w_lo, y2_hi), (w_hi, y2_lo))):
                        if first and n == 2:
                            wait(pe, y2_lo_ready, i, 2, h + 1)
                        last = mm(dst[:, h * HALF:(h + 1) * HALF], wt[:, w:w + P],
                                  y[:, i[0] % 2, h * HALF:(h + 1) * HALF], start=(n == 0), stop=(n == 2))
                return last

            def key(i, ch):
                wait(pe, relu_done, i, CHUNKS, ch - 1)
                project(kps[ch % 2], i, ch * P, ch == 0).then_inc(key_done, 1)

            def value(i, ch, halves=(0, 1)):
                wait(pe, sq_done, i, CHUNKS, ch + 1)
                if ch == 0:
                    wait(pe, rk_ready, at(i, -1))
                for h in halves:
                    last = mm(kv[:, h * HALF:(h + 1) * HALF], col("w_value")[:, ch * P:(ch + 1) * P],
                              hid[:, ch, h * HALF:(h + 1) * HALF], start=(ch == 0), stop=(ch == CHUNKS - 1))
                if halves[-1] == 1:
                    last.then_inc(value_done, 1)

            def step(i):
                f, e, b, c = at(i, 2), at(i, 1), at(i, -1), at(i, -2)
                if real(i):
                    key(i, 1)
                if real(c):
                    wait(pe, z_ready[3], c)
                    turn_all(lambda g: z3[:, g, :], z3_turned,
                             (t1_ready, at(f, -1)), (recep_ready, at(i, -1)), (lg_ready, at(c, -1)), halves=(1, 0))
                if real(i):
                    value(i, 0)
                if real(b):
                    wait(pe, rk_ready, b)
                    turn_all(lambda g: rk[:, g * P:(g + 1) * P], rk_turned, (tn_ready, c), (t1_ready, at(f, -1)))
                if real(i):
                    key(i, 2)
                    value(i, 1)
                if real(e):
                    wait(pe, z_ready[2], e)
                    turn_all(lambda g: z2[:, g, :], z2_turned, (x1_ready, b), (t1_ready, at(f, -1)))
                if real(i):
                    key(i, 3)
                    value(i, 2, (0,))
                if real(f):
                    wait(pe, z_ready[1], f)
                    turn_all(lambda g: z1[:, g, :], z1_turned, (y2_lo_ready, e))
                if real(i):
                    value(i, 2, (1,))
                    value(i, 3, (0,))
                if real(c):
                    wait(pe, tn_ready, c)
                    wait_first(0, (y1_ready, f), (y2_lo_ready, e), (x1_ready, b))
                    for h in range(2):
                        last = mm(ms[h * EXPERTS:(h + 1) * EXPERTS, 0:HALF], w_gate[:, :],
                                  tn[:, h * HALF:(h + 1) * HALF], start=True, stop=True)
                    last.then_inc(gate_done, 1)
                if real(i):
                    value(i, 3, (1,))
                    wait_first(1, (y1_ready, f), (y2_lo_ready, e), (x1_ready, b))
                    project(ms, i, HID, False, (1,)).then_inc(recep_done, 1)
                    wait_first(0, (lg_ready, c))
                    project(ms, i, HID, False, (0,)).then_inc(recep_done, 1)
                if real(e):
                    wait(pe, y2_ready, e, 2)
                    key(e, 0)
                if real(f):
                    wait(pe, silu_ready, f)
                    for h in (1, 0):
                        wait_first(h, (recep_ready, i), (y1_ready, f))
                        for g in range(h * GROUPS // 2, (h + 1) * GROUPS // 2):
                            last = mm(ms[:, g * P:(g + 1) * P], sl[:, g * P:(g + 1) * P], col("w_out"),
                                      start=True, stop=True)
                        last.then_inc(att_done, 1)

            pe.wait_ge(cst_loaded, 16)
            mm(kps[0][:, 0:HID], col("w_whiten"), col("w_key"), start=True, stop=True)
            mm(kps[0][:, HID:HID + P], col("w_whiten"), col("w_recep"), start=True, stop=True).then_inc(fold_mm, 1)
            pe.wait_ge(fold_raw, 3)
            for ch in range(CHUNKS + 1):
                last = mm(ms[:, ch:ch + 1], hid[:, 0, ch * P:(ch + 1) * P], col("b2"), start=True, stop=True)
            last.then_inc(fold_bias, 1)
            pe.wait_ge(fold_centre, 1)
            mm(kps[1][:, 0:HID], centre[:, :], hid[:, 1, 0:HID], start=True, stop=True)
            mm(kps[1][:, HID:HID + P], centre[:, :], hid[:, 1, HID:HID + P], start=True, stop=True)
            mm(kv[:, 0:EXPERTS], centre[:, :], col("gate_w"), start=True, stop=True).then_inc(fold_mm2, 1)
            pe.wait_ge(fold_ready, 6)
            pe.wait_ge(fold_lo, 1)
            run_steps(pe, step)

            pe.wait_ge(rowb_ready, 1)
            for q in range(2):
                for k in range(TOPK):
                    last = turn(kps[q][:, k * P:(k + 1) * P], row_b[:, q * TOPK + k, :], ident[:, :])
                last.then_inc(row_turned, 1)
            for q in range(2):
                pe.wait_ge(pooling, q + 1)
                last = turn(ms[:, q * P:(q + 1) * P], pooled[:, q, 0, :], ident[:, :])
            last.then_inc(pool_turned, 1)
            pe.wait_ge(pooled_ready, 1)

            def up(g):
                pe.wait_ge(lot_loaded[g % RING][0], 16 * (g // RING + 1))
                if g >= 2:
                    pe.wait_ge(up_copied, g - 1)
                for e in range(FG):
                    last = mm(kv[32 * e:32 * e + BATCH, HALF * (g % 2):HALF * (g % 2 + 1)],
                              pooled_t[:, :, g * FG + e], ring[g % RING][0][:, e * FFN:(e + 1) * FFN],
                              start=True, stop=True)
                last.then_inc(up_done, 1)

            def turn_up(g):
                pe.wait_ge(up_copied, g + 1)
                if g >= 2:
                    pe.wait_ge(pre_ready, g - 1)
                else:
                    pe.wait_ge(row_copied, 2)
                for f in range(FC):
                    o = HALF * (g % 2) + f * P
                    last = turn(kps[0][:, o:o + P], up_sb[:, g % 2, f * P:(f + 1) * P], ident[:, :])
                last.then_inc(up_turned, 1)

            def down(g):
                pe.wait_ge(lot_loaded[g % RING][1], 16 * (g // RING + 1))
                pe.wait_ge(gelu_ready, g + 1)
                dst, o = (kps[1], ms)[g // (LOTS // 2)], g % (LOTS // 2) * P
                for e in range(FG):
                    for f in range(FC):
                        w = (e * FC + f) * P
                        last = mm(dst[32 * e:32 * e + BATCH, o:o + P],
                                  hact[:, g % 2, (f * FG + e) * BATCH:(f * FG + e + 1) * BATCH],
                                  ring[g % RING][1][:, w:w + P], start=(f == 0), stop=(f == FC - 1))
                last.then_inc(down_done, 1)

            for g in range(LOTS + 2):
                if g < LOTS:
                    up(g)
                if 1 <= g <= LOTS:
                    turn_up(g - 1)
                if g >= 2:
                    down(g - 2)
            pe.wait_ge(pre_ready, LOTS)
            for n, dst in enumerate((kv, kps[0])):
                pe.wait_ge(down_copied, n + 1)
                for g in range(LOTS // 2):
                    last = turn(dst[:, g * P:(g + 1) * P], down_sb[n][:, g, :], ident[:, :])
            last.then_inc(ffn_turned, 1)
            pe.wait_ge(ffnt_ready, 1)
            for q in range(2):
                last = turn(ms[:, q * P:(q + 1) * P],
                            ffn_t[:, :, :].rearrange("p b e -> p (b e)")[:, q * P:(q + 1) * P], ident[:, :])
            last.then_inc(ffn_turned, 1)
            pe.wait_ge(ffno_ready, 1)
            for q in range(2):
                for k in range(TOPK):
                    last = mm(kps[q][:, k * P:(k + 1) * P], share[:, q, k * P:(k + 1) * P], ffn_o[:, q, :],
                              start=True, stop=True)
                last.then_inc(added_done, 1)


def kernel(**inputs):
    import numpy as np
    import concourse.bacc as bacc
    from concourse.bass_utils import run_bass_kernel_spmd

    a = {k: np.asarray(v) for k, v in inputs.items()}

    t = a["x"].reshape(2, 2, P, PAIR_UNITS, HALF // P, P).transpose(0, 3, 5, 1, 4, 2)
    x = np.ascontiguousarray(t).reshape(UNITS, P, GROUPS * P)

    c = np.empty((P, COLS), np.float32)
    parts = {
        "g0": np.broadcast_to(a["L0_conv_ln0_g"], (P, P)), "b0": np.broadcast_to(a["L0_conv_ln0_b"], (P, P)),
        "w_out": a["L0_conv_W_out"].T, "w_whiten": a["L0_conv_W_whiten"], "w_key": a["L0_conv_W_key"].T,
        "w_recep": a["L0_conv_W_recep"].T,
        "w_value": a["L0_conv_W_value"].T.reshape(CHUNKS, P, P).transpose(1, 0, 2).reshape(P, HID),
        "gate_w": a["L0_ffn_gate_w"].T, "g1": a["L0_conv_ln1_g"][:, None], "b1": a["L0_conv_ln1_b"][:, None],
        "g2": a["L0_conv_ln2_g"][:, None], "b2": a["L0_conv_ln2_b"][:, None],
        "gate_b": np.concatenate([a["L0_ffn_gate_b"]] * 2)[:, None],
        "ffn_b1": a["L0_ffn_weight1"][:, P, :].reshape(EXPERTS, FC, P).transpose(2, 0, 1).reshape(P, EXPERTS * FC),
        "ffn_b2": a["L0_ffn_weight2"][:, FFN, :].T,
    }
    for name, value in parts.items():
        c[:, COL[name][0]:COL[name][1]] = value

    w1 = a["L0_ffn_weight1"][:, :P, :].reshape(LOTS, FG, P, FFN).transpose(0, 2, 1, 3).reshape(LOTS, P, FG * FFN)
    w2 = a["L0_ffn_weight2"][:, :FFN, :].reshape(LOTS, FG, FC, P, P).transpose(0, 3, 1, 2, 4)
    wff = np.concatenate([w1, w2.reshape(LOTS, P, FG * FFN)], axis=2)

    nc = bacc.Bacc("TRN2", target_bir_lowering=False, num_devices=1)
    arrays = {"x_dram": x, "cst_dram": c, "wff_dram": np.ascontiguousarray(wff)}
    args = [nc.dram_tensor(n, v.shape, mybir.dt.from_np(v.dtype), kind="ExternalInput").ap() for n, v in arrays.items()]
    names = ("out0_dram", "out1_dram")
    outs = [nc.dram_tensor(n, (PAIR_UNITS, P, GROUPS * P), F32, kind="ExternalOutput").ap() for n in names]
    metaformer_kernel(nc, *args, outs)
    results = run_bass_kernel_spmd(nc, [arrays], core_ids=[0]).results[0]
    y = np.stack([np.asarray(results[n]) for n in names]).reshape(2, PAIR_UNITS, P, 2, HALF // P, P).transpose(0, 3, 5, 1, 4, 2)
    return np.ascontiguousarray(y).reshape(BATCH, P, P, P)
```
